# Optimizing a Trainium2 kernel written in Bass

```python
import numpy as np
import jax
import jax.numpy as jnp

def _softmax(x, axis=-1):
    return jax.nn.softmax(x, axis=axis)

def _gelu(x):
    return jax.nn.gelu(x, approximate=True)

def _silu(x):
    return jax.nn.silu(x)

def _sigmoid(x):
    return jax.nn.sigmoid(x)

def _layernorm(x, axis=-1, eps=1e-05):
    m = jnp.mean(x, axis=axis, keepdims=True)
    v = jnp.var(x, axis=axis, keepdims=True)
    return (x - m) / jnp.sqrt(v + eps)

def _scatter_add(tgt, idx, src, axis=0):
    return tgt.at[idx].add(src)

def _segment_sum(src, seg, n):
    return jax.ops.segment_sum(src, seg, n)
kernel_name = 'mk_seq_preln_d1_jaxref_r8_6b3ecd'

def setup_inputs(seed: int=0):
    np.random.seed(seed)
    _w = jnp.asarray

    def _L0_attn_setup():
        import jax, jax.numpy as jnp
        import numpy as np
        B, T, HID = (1, 128, 256)
        H, DK, DV, M, KW = (16, 128, 128, 128, 4)
        SCALE = DK ** (-0.5)
        EPS = 1e-05

        def short_conv(x, w):
            K = w.shape[1]
            xp = jnp.pad(x, ((0, 0), (K - 1, 0), (0, 0)))
            t = x.shape[1]
            y = sum((xp[:, i:i + t] * w[:, i] for i in range(K)))
            return jax.nn.silu(y)

        def l2norm(x):
            return x * jax.lax.rsqrt(jnp.sum(x * x, axis=-1, keepdims=True) + 1e-06)

        def gsa2_scan(q, k, v, w, g, beta):
            b = q.shape[0]
            tm = lambda x: jnp.moveaxis(x, 1, 0)
            Sk0 = jnp.zeros((b, H, DK, M), q.dtype)
            Sv0 = jnp.zeros((b, H, M, DV), q.dtype)

            def step(carry, xs):
                Sk, Sv = carry
                q_t, k_t, v_t, w_t, g_t, b_t = xs
                gt = jnp.exp(g_t)
                bw = b_t[:, :, None] * w_t
                Sk = Sk * gt[:, :, None, :] + k_t[..., :, None] * bw[:, :, None, :]
                Sv = Sv * gt[..., None] + bw[..., None] * v_t[:, :, None, :]
                s = jnp.einsum('bhd,bhdm->bhm', q_t, Sk) * SCALE
                a = jax.nn.softmax(s, axis=-1)
                o_t = jnp.einsum('bhm,bhmd->bhd', a, Sv)
                return ((Sk, Sv), o_t)
            (_, _), o = jax.lax.scan(step, (Sk0, Sv0), (tm(q), tm(k), tm(v), tm(w), tm(g), tm(beta)))
            return jnp.moveaxis(o, 0, 1)
        key = jax.random.key(seed)
        ks = jax.random.split(key, 16)
        s = 0.02
        return {'hidden_states': jax.random.normal(ks[0], (B, T, HID), jnp.float32), 'Wq': jax.random.normal(ks[1], (HID, H * DK), jnp.float32) * s, 'Wk': jax.random.normal(ks[2], (HID, H * DK), jnp.float32) * s, 'Wv': jax.random.normal(ks[3], (HID, H * DV), jnp.float32) * s, 'Ww': jax.random.normal(ks[4], (HID, H * M), jnp.float32) * s, 'cq': jax.random.normal(ks[5], (H * DK, KW), jnp.float32) * 0.2, 'ck': jax.random.normal(ks[6], (H * DK, KW), jnp.float32) * 0.2, 'cv': jax.random.normal(ks[7], (H * DV, KW), jnp.float32) * 0.2, 'Wf1': jax.random.normal(ks[8], (HID, DV), jnp.float32) * s, 'Wf2': jax.random.normal(ks[9], (DV, H * M), jnp.float32) * s, 'Wb': jax.random.normal(ks[10], (HID, H), jnp.float32) * s, 'Wg1': jax.random.normal(ks[11], (HID, DV), jnp.float32) * s, 'Wg2': jax.random.normal(ks[12], (DV, H * DV), jnp.float32) * s, 'bg2': jnp.zeros((H * DV,), jnp.float32), 'norm_w': jnp.ones((DV,), jnp.float32), 'Wo': jax.random.normal(ks[13], (H * DV, HID), jnp.float32) * s}
    _L0_attn_in = _L0_attn_setup()

    def _L0_ffn_setup():
        import jax, jax.numpy as jnp
        import numpy as np
        FP8_MAX = 448.0
        SCALE_MARGIN = 0.8

        def _fp8_quant_dequant(t, scale):
            q = (t / scale).astype(jnp.float8_e4m3fn)
            return q.astype(jnp.float32) * scale
        key = jax.random.key(seed)
        k1, k2 = jax.random.split(key)
        B, S, D_IN, D_OUT = (4, 256, 256, 256)
        x = jax.random.normal(k1, (B, S, D_IN), dtype=jnp.float32)
        weight = jax.random.normal(k2, (D_OUT, D_IN), dtype=jnp.float32)
        bias = jnp.zeros((D_OUT,), dtype=jnp.float32)
        return {'x': x, 'weight': weight, 'bias': bias}
    _L0_ffn_in = _L0_ffn_setup()
    _d = {'L0_attn_hidden_states': _L0_attn_in['hidden_states'], 'L0_attn_Wq': _L0_attn_in['Wq'], 'L0_attn_Wk': _L0_attn_in['Wk'], 'L0_attn_Wv': _L0_attn_in['Wv'], 'L0_attn_Ww': _L0_attn_in['Ww'], 'L0_attn_cq': _L0_attn_in['cq'], 'L0_attn_ck': _L0_attn_in['ck'], 'L0_attn_cv': _L0_attn_in['cv'], 'L0_attn_Wf1': _L0_attn_in['Wf1'], 'L0_attn_Wf2': _L0_attn_in['Wf2'], 'L0_attn_Wb': _L0_attn_in['Wb'], 'L0_attn_Wg1': _L0_attn_in['Wg1'], 'L0_attn_Wg2': _L0_attn_in['Wg2'], 'L0_attn_bg2': _L0_attn_in['bg2'], 'L0_attn_norm_w': _L0_attn_in['norm_w'], 'L0_attn_Wo': _L0_attn_in['Wo'], 'L0_ffn_weight': _L0_ffn_in['weight'], 'L0_ffn_bias': _L0_ffn_in['bias']}
    _x0 = _d['L0_attn_hidden_states']
    _d['L0_attn_hidden_states'] = jax.random.normal(jax.random.fold_in(jax.random.key(seed), 1), (2, 2048, 256), dtype=_x0.dtype)
    del _x0
    return _d

def reference(L0_attn_hidden_states, L0_attn_Wq, L0_attn_Wk, L0_attn_Wv, L0_attn_Ww, L0_attn_cq, L0_attn_ck, L0_attn_cv, L0_attn_Wf1, L0_attn_Wf2, L0_attn_Wb, L0_attn_Wg1, L0_attn_Wg2, L0_attn_bg2, L0_attn_norm_w, L0_attn_Wo, L0_ffn_weight, L0_ffn_bias):

    def _L0_attn_ref(hidden_states, Wq, Wk, Wv, Ww, cq, ck, cv, Wf1, Wf2, Wb, Wg1, Wg2, bg2, norm_w, Wo):
        import jax, jax.numpy as jnp
        import numpy as np
        B, T, HID = (1, 128, 256)
        H, DK, DV, M, KW = (16, 128, 128, 128, 4)
        SCALE = DK ** (-0.5)
        EPS = 1e-05

        def short_conv(x, w):
            K = w.shape[1]
            xp = jnp.pad(x, ((0, 0), (K - 1, 0), (0, 0)))
            t = x.shape[1]
            y = sum((xp[:, i:i + t] * w[:, i] for i in range(K)))
            return jax.nn.silu(y)

        def l2norm(x):
            return x * jax.lax.rsqrt(jnp.sum(x * x, axis=-1, keepdims=True) + 1e-06)

        def gsa2_scan(q, k, v, w, g, beta):
            b = q.shape[0]
            tm = lambda x: jnp.moveaxis(x, 1, 0)
            Sk0 = jnp.zeros((b, H, DK, M), q.dtype)
            Sv0 = jnp.zeros((b, H, M, DV), q.dtype)

            def step(carry, xs):
                Sk, Sv = carry
                q_t, k_t, v_t, w_t, g_t, b_t = xs
                gt = jnp.exp(g_t)
                bw = b_t[:, :, None] * w_t
                Sk = Sk * gt[:, :, None, :] + k_t[..., :, None] * bw[:, :, None, :]
                Sv = Sv * gt[..., None] + bw[..., None] * v_t[:, :, None, :]
                s = jnp.einsum('bhd,bhdm->bhm', q_t, Sk) * SCALE
                a = jax.nn.softmax(s, axis=-1)
                o_t = jnp.einsum('bhm,bhmd->bhd', a, Sv)
                return ((Sk, Sv), o_t)
            (_, _), o = jax.lax.scan(step, (Sk0, Sv0), (tm(q), tm(k), tm(v), tm(w), tm(g), tm(beta)))
            return jnp.moveaxis(o, 0, 1)
        h = hidden_states
        q = short_conv(h @ Wq, cq)
        k = short_conv(h @ Wk, ck)
        v = short_conv(h @ Wv, cv)
        w = short_conv(h @ Ww, cv)
        g = jax.nn.log_sigmoid(h @ Wf1 @ Wf2)
        beta = jax.nn.sigmoid(h @ Wb)
        rs = lambda x, d: x.reshape(x.shape[0], x.shape[1], -1, d)
        q, k = (rs(q, DK), rs(k, DK))
        v = rs(v, DV)
        w = l2norm(rs(w, M))
        g = rs(g, M)
        o = gsa2_scan(q, k, v, w, g, beta)
        gate = rs(h @ Wg1 @ Wg2 + bg2, DV)
        o = o * jax.lax.rsqrt(jnp.mean(o * o, axis=-1, keepdims=True) + EPS)
        o = o * norm_w * jax.nn.sigmoid(gate)
        o = o.reshape(o.shape[0], o.shape[1], -1)
        return o @ Wo

    def _L0_ffn_ref(x, weight, bias):
        import jax, jax.numpy as jnp
        import numpy as np
        FP8_MAX = 448.0
        SCALE_MARGIN = 0.8

        def _fp8_quant_dequant(t, scale):
            q = (t / scale).astype(jnp.float8_e4m3fn)
            return q.astype(jnp.float32) * scale
        amax_x = jnp.max(jnp.abs(x))
        amax_w = jnp.max(jnp.abs(weight))
        x_scale = amax_x / (FP8_MAX * SCALE_MARGIN)
        w_scale = jnp.maximum(amax_x, amax_w) / (FP8_MAX * SCALE_MARGIN)
        x_scale = jax.lax.stop_gradient(x_scale)
        w_scale = jax.lax.stop_gradient(w_scale)
        x_dq = _fp8_quant_dequant(x, x_scale)
        w_dq = _fp8_quant_dequant(weight, w_scale)
        out = jnp.einsum('bsd,od->bso', x_dq, w_dq)
        return out + bias
    x = L0_attn_hidden_states
    x = x + _L0_attn_ref(_layernorm(x, axis=-1), L0_attn_Wq, L0_attn_Wk, L0_attn_Wv, L0_attn_Ww, L0_attn_cq, L0_attn_ck, L0_attn_cv, L0_attn_Wf1, L0_attn_Wf2, L0_attn_Wb, L0_attn_Wg1, L0_attn_Wg2, L0_attn_bg2, L0_attn_norm_w, L0_attn_Wo)
    x = x + _L0_ffn_ref(_layernorm(x, axis=-1), L0_ffn_weight, L0_ffn_bias)
    return x

_drawn_inputs = setup_inputs


def setup_inputs(seed=0):
    import zlib

    import numpy as np

    out = dict(_drawn_inputs(seed))
    spreads = {'L0_attn_bg2': (0.0, 0.566), 'L0_attn_norm_w': (1.0, 0.573), 'L0_ffn_bias': (0.0, 0.8)}
    factors = {'L0_attn_Wq': 8.0,
     'L0_attn_Wk': 8.0,
     'L0_attn_cq': 8.0,
     'L0_attn_ck': 8.0,
     'L0_attn_Wf1': 8.0,
     'L0_attn_Wf2': 8.0,
     'L0_attn_Wb': 2.862,
     'L0_attn_Wg1': 6.481,
     'L0_attn_Wg2': 5.711}
    for name, (base, spread) in spreads.items():
        noise = np.random.default_rng([zlib.crc32(name.encode()), seed]).standard_normal(out[name].shape)
        drawn = base * np.exp(spread * noise) if base else spread * noise
        out[name] = jnp.asarray(drawn.astype(out[name].dtype))
    for name, factor in factors.items():
        out[name] = (out[name] * factor).astype(out[name].dtype)
    return out
```

```python
from contextlib import ExitStack

import concourse.bass as bass
from concourse import mybir

ALU = mybir.AluOpType
ACT = mybir.ActivationFunctionType
F32 = mybir.dt.float32
BF16 = mybir.dt.bfloat16
U32 = mybir.dt.uint32
AX = mybir.AxisListType
RMAX = bass.bass_isa.ReduceOp.max

P = 128
HID = 256
KT = HID // P
H = 16
TOK = 4096
SEQ = 2048
C = 4
NT = C * P
BLOCKS = TOK // NT
UN = SEQ // NT
GROUPS = H * TOK // SEQ
CHUNKS = TOK // P
TAPS = 4
LEVELS = (64, 32, 16, 8)
DIAG = 8
REF = DIAG // 2 - 1
ZMIN = -20.0
SCALE = float(P) ** -0.5
SC = SCALE / 4.0
EPS = 1e-5
L2EPS = 1e-6
QMAX = 448.0 * 0.8

NR = 4 * 64
INCL, DPOS, RIGHT = 0, P, 2 * P
SUF, LEFT, DNEG = 0, P, P + NR


class Steps:

    def __init__(self, handle, per):
        self.handle, self.per = handle, per

    def at(self, g, blk, k):
        return g * (UN * self.per) + (blk + 2) * self.per + k


def program(nc, x_d, wqkvw_d, conv_d, wf1_d, wf2_d, wb_d, wg1_d, wg2_d, bg_d, nw_d, wo_d, fw_d, fb_d,
            msum_d, mask_d, perm_d, eye_d, out_d, hT_d, h1_d, g_d):
    ctx = ExitStack()
    with ctx:
        def sb(name, shape, dt=F32, stack=ctx):
            return stack.enter_context(nc.sbuf_tensor(name, shape, dt))

        def sem(name):
            return ctx.enter_context(nc.semaphore(name))

        def steps(name, per):
            return Steps(sem(name), per)

        bank = [ctx.enter_context(nc.psum_tensor(f"bank{i}", [P, 512], F32)) for i in range(8)]
        X, L, Z, S, O = bank[0:2], bank[2:4], bank[4:6], bank[6], bank[7]

        xa = sb("xa", [P, CHUNKS, HID])
        msum = sb("msum", [P, 896])
        mask = sb("mask", [P, 384])
        perm = sb("perm", [P, 2, P])
        eye = sb("eye", [P, P])
        eyeb = sb("eyeb", [P, P], BF16)
        ones = sb("ones", [P, 1])
        half = sb("half", [P, 4])
        beta = sb("beta", [P, H, CHUNKS])
        nwh = sb("nwh", [P, 1])
        nw = sb("nw", [P, 1])

        const_in = sem("const_in")
        x_in = sem("x_in")
        ones_set = sem("ones_set")
        pr_stat = sem("pr_stat")
        pr_aggr = sem("pr_aggr")
        pr_var = sem("pr_var")
        pr_rstd = sem("pr_rstd")
        pr_h = sem("pr_h")
        pr_tr = sem("pr_tr")
        pr_hT = sem("pr_hT")
        pr_low = sem("pr_low")
        pr_lowc = sem("pr_lowc")
        pr_beta = sem("pr_beta")
        pr_betac = sem("pr_betac")
        pr_z = sem("pr_z")
        pr_zc = sem("pr_zc")
        pr_exp = sem("pr_exp")
        pr_ln = sem("pr_ln")
        pr_st = sem("pr_st")
        pr_sg = sem("pr_sg")
        pr_tanh = sem("pr_tanh")
        pr_bset = sem("pr_bset")

        ht_in = [sem(f"ht_in{i}") for i in range(2)]
        g_in = [sem(f"g_in{i}") for i in range(2)]
        h1_in = [sem(f"h1_in{i}") for i in range(2)]
        w_in = sem("w_in")
        w2_in = sem("w2_in")
        proj = steps("proj", 4)
        halo = steps("halo", 4)
        pevac = steps("pevac", 8)
        conv = steps("conv", 12)
        tanh = steps("tanh", 4)
        silu = steps("silu", 4)
        packs = steps("packs", 12)
        wsq = steps("wsq", 1)
        wss = steps("wss", 1)
        cv = steps("cv", 1)
        cpow = steps("cpow", 1)
        cnat = steps("cnat", 1)
        cperm = steps("cperm", 1)
        call = steps("call", 2)
        mcs = steps("mcs", 1)
        lsum = steps("lsum", 8)
        expA = steps("expA", 8)
        expB = steps("expB", 4)
        wprod = steps("wprod", 6)
        utr = steps("utr", 4)
        uevac = steps("uevac", 8)
        kvtr = steps("kvtr", 4)
        kvevac = steps("kvevac", 4)
        stps = steps("stps", 4)
        st0 = steps("st0", 1)
        stupd = steps("stupd", 4)
        sktr = steps("sktr", 1)
        skevac = steps("skevac", 1)
        qk = steps("qk", 4)
        aevac = steps("aevac", 4)
        sc = steps("sc", 4)
        prods = steps("prods", 4)
        adds = steps("adds", 5)
        strn = steps("strn", 1)
        smax = steps("smax", 1)
        nmax = steps("nmax", 1)
        sexp = steps("sexp", 4)
        atrn = steps("atrn", 1)
        aes = steps("aes", 5)
        pps = steps("pps", 4)
        pevc = steps("pevc", 4)
        ops = steps("ops", 1)
        gps = steps("gps", 1)
        gth = steps("gth", 1)
        osqs = steps("osqs", 1)
        ogs = steps("ogs", 1)
        rss = steps("rss", 1)
        rsv = steps("rsv", 2)
        rpow = steps("rpow", 1)
        wops = steps("wops", 2)
        oacc = steps("oacc", 4)
        wos_set = sem("wos_set")

        f_in = sem("f_in")
        f_stat = sem("f_stat")
        f_aggr = sem("f_aggr")
        f_var = sem("f_var")
        f_rstd = sem("f_rstd")
        f_y = sem("f_y")
        f_mx = sem("f_mx")
        f_wmx = sem("f_wmx")
        f_amax = sem("f_amax")
        f_all = sem("f_all")
        f_sc = sem("f_sc")
        f_q = sem("f_q")
        f_wq = sem("f_wq")
        f_tr = sem("f_tr")
        f_trc = sem("f_trc")
        f_mm = sem("f_mm")
        f_out = sem("f_out")
        f_xb = sem("f_xb")
        f_st = sem("f_st")

        pro = ExitStack()
        wf1 = sb("wf1", [P, KT, P], stack=pro)
        wg1 = sb("wg1", [P, KT, P], stack=pro)
        wf2 = sb("wf2", [P, H * P], stack=pro)
        wb = sb("wb", [P, KT, H], stack=pro)
        stat = sb("stat", [P, C, 6], stack=pro)
        mv = sb("mv", [P, C, 2], stack=pro)
        var = sb("var", [P, C], stack=pro)
        rstd = sb("rstd", [P, C], stack=pro)
        hn = sb("hn", [P, C, HID], stack=pro)
        hTb = sb("hTb", [P, KT, NT], stack=pro)
        low = sb("low", [P, 2, NT], stack=pro)
        zs = sb("zs", [P, C, H * P], stack=pro)
        braw = sb("braw", [P, H, CHUNKS], stack=pro)
        pro.close()

        mn = ExitStack()
        hT = sb("hT", [P, 2, KT, NT], stack=mn)
        h1 = sb("h1", [P, 2, NT], stack=mn)
        gl = sb("gl", [P, 2, NT], stack=mn)
        wh = sb("wh", [P, KT, 4, P], stack=mn)
        cw = sb("cw", [P, 4, TAPS], stack=mn)
        wg2 = sb("wg2", [P, P], stack=mn)
        wo = sb("wo", [P, HID], stack=mn)
        wos = sb("wos", [P, HID], stack=mn)
        bg = sb("bg", [P, 1], stack=mn)
        bgh = sb("bgh", [P, 1], stack=mn)
        xb = sb("xb", [P, 4, NT + 4], stack=mn)
        y = sb("y", [P, 4, NT], stack=mn)
        th = sb("th", [P, 2, NT], stack=mn)
        pk = sb("pk", [P, 3, C, NR], stack=mn)
        ysq = sb("ysq", [P, NT], stack=mn)
        cvv = sb("cvv", [P, C], stack=mn)
        cpw = sb("cpw", [P, C], stack=mn)
        cc = sb("cc", [P, 3, C], stack=mn)
        mc = sb("mc", [P, C, 384], stack=mn)
        ER = sb("ER", [P, C, 512], stack=mn)
        EL = sb("EL", [P, C, 512], stack=mn)
        U = sb("U", [P, C, 512], stack=mn)
        kv = sb("kv", [P, C, 512], stack=mn)
        ST = sb("ST", [P, C + 1, 2 * P], stack=mn)
        Sk = sb("Sk", [P, C, P], stack=mn)
        A = sb("A", [P, C, 384], stack=mn)
        pr = sb("pr", [P, C, 512], stack=mn)
        mx = sb("mx", [P, C], stack=mn)
        nm = sb("nm", [P, C], stack=mn)
        den = sb("den", [P, C], stack=mn)
        a = sb("a", [P, C, P], stack=mn)
        Pm = sb("Pm", [P, C, 384], stack=mn)
        gt = sb("gt", [P, NT], stack=mn)
        AE = A_E = sb("AE", [P, C, 512], stack=mn)
        osq = ysq2 = sb("osq", [P, NT], stack=mn)
        og = sb("og", [P, NT], stack=mn)
        r0 = sb("r0", [P, C], stack=mn)
        r1 = sb("r1", [P, C], stack=mn)
        rr = sb("rr", [P, C], stack=mn)
        mn.close()

        ff = ExitStack()
        fy = sb("fy", [P, CHUNKS, HID], stack=ff)
        fq = sb("fq", [P, CHUNKS, HID], BF16, stack=ff)
        fu = sb("fu", [P, C * HID], stack=ff)
        fm = sb("fm", [P, C * HID], stack=ff)
        fstat = sb("fstat", [P, C, 6], stack=ff)
        fmv = sb("fmv", [P, C, 2], stack=ff)
        fvar = sb("fvar", [P, C], stack=ff)
        frstd = sb("frstd", [P, C], stack=ff)
        fhi = sb("fhi", [P, BLOCKS], stack=ff)
        flo = sb("flo", [P, BLOCKS], stack=ff)
        fw = sb("fw", [P, KT, HID], stack=ff)
        fwq = sb("fwq", [P, KT, HID], BF16, stack=ff)
        fwT = sb("fwT", [P, KT, HID], BF16, stack=ff)
        fb = sb("fb", [P, HID], stack=ff)
        fs = sb("fs", [P, 16], stack=ff)
        fqT = sb("fqT", [P, C, KT, P], BF16, stack=ff)
        fo = sb("fo", [P, 2, C, HID], stack=ff)
        ff.close()

        passed = {name: sem("passed_" + name) for name in ("sp", "dve", "pool")}

        def hold(eng, name, handle, value):
            eng.wait_ge(handle, value)
            eng.sem_inc(passed[name], 1)

        block = ctx.enter_context(nc.Block())

        def left(t, s):
            return t.rearrange("p (c n two s) -> p c n two s", c=C, two=2, s=s)[:, :, :, 0, :]

        def right(t, s):
            return t.rearrange("p (c n two s) -> p c n two s", c=C, two=2, s=s)[:, :, :, 1, :]

        def packed(t, col, s):
            return t[:, :, col:col + 64].rearrange("p c (n s) -> p c n s", s=s)

        def par(blk):
            return blk % 2

        def loads(g, blk):
            return g * (16 * UN // 2) + 16 * (blk // 2 + 1)

        def run(eng, slot, first):
            first()
            with eng.Fori(0, GROUPS - 1) as g:
                for blk in range(UN):
                    slot(g, blk, True)
            for blk in range(UN):
                slot(GROUPS - 1, blk, blk < UN - 1)

        @block.sync
        def _(sp):
            for dst, src in ((msum, msum_d), (mask, mask_d), (perm, perm_d), (eye, eye_d), (nw, nw_d),
                             (wf1, wf1_d), (wg1, wg1_d), (wf2, wf2_d), (wb, wb_d)):
                sp.dma_start(dst[:], src).then_inc(const_in, 16)
            with sp.Fori(0, BLOCKS) as i:
                sp.dma_start(xa[:, bass.ds(i * C, C), :],
                             x_d[bass.ds(i * NT, NT), :].rearrange("(c p) d -> p c d", p=P)).then_inc(x_in, 16)
                hold(sp, "sp", x_in, i * 16 + 16)
            with sp.Fori(0, BLOCKS) as i:
                hold(sp, "sp", pr_hT, i * 2 + 2)
                sp.dma_start(hT_d[bass.ds(i, 1)].rearrange("o p n -> (o p) n"),
                             hTb[:].rearrange("p k n -> p (k n)")).then_inc(pr_st, 16)
                hold(sp, "sp", pr_lowc, i * 2 + 2)
                sp.dma_start(h1_d[bass.ds(i, 1)].rearrange("o p n -> (o p) n"), low[:, 1, :]).then_inc(pr_st, 16)
                hold(sp, "sp", pr_ln, i * 16 + 16)
                for b in range(2):
                    for c in range(C):
                        sp.dma_start(
                            g_d[b * 8:b * 8 + 8, bass.ds(i, 1), :, c * P:(c + 1) * P].rearrange(
                                "h o p m -> (o p) h m"),
                            zs[:, c, b * 8 * P:(b + 1) * 8 * P].rearrange("p (h m) -> p h m", m=P)
                        ).then_inc(pr_sg, 16)
            hold(sp, "sp", pr_st, BLOCKS * 32)
            hold(sp, "sp", pr_sg, BLOCKS * 128)
            hold(sp, "sp", pr_bset, 1)

            def load_block(g, blk, static):
                p = par(blk)
                n8 = (g % 2) * UN + blk if static else (g % 2) * UN + blk
                hold(sp, "sp", proj.handle, proj.at(g, blk - 2, 4))
                sp.dma_start(hT[:, p].rearrange("p k n -> p (k n)"),
                             hT_d[bass.ds(n8, 1)].rearrange("o p n -> (o p) n")).then_inc(ht_in[p], 16)
                hold(sp, "sp", lsum.handle, lsum.at(g, blk - 2, 8))
                hh = g // 2
                sp.dma_start(gl[:, p, :],
                             g_d[bass.ds(hh, 1), bass.ds(n8, 1)].rearrange("a o p m -> (a o p) m")
                             ).then_inc(g_in[p], 16)
                if blk == 0:
                    hold(sp, "sp", proj.handle, proj.at(g, -1, 4))
                    hold(sp, "sp", conv.handle, conv.at(g, -1, 12))
                    sp.dma_start(wh[:].rearrange("p k a n -> p (k a n)"),
                                 wqkvw_d[bass.ds(hh, 1)].rearrange("o p n -> (o p) n")).then_inc(w_in, 16)
                    sp.dma_start(cw[:].rearrange("p a t -> p (a t)"),
                                 conv_d[bass.ds(hh, 1)].rearrange("o p n -> (o p) n")).then_inc(w_in, 16)
                    hold(sp, "sp", wops.handle, wops.at(g, -1, 2))
                    hold(sp, "sp", gth.handle, gth.at(g, -1, 1))
                    for dst, src in ((wg2, wg2_d), (wo, wo_d), (bg, bg_d)):
                        sp.dma_start(dst[:], src[bass.ds(hh, 1)].rearrange("o p n -> (o p) n")
                                     ).then_inc(w2_in, 16)
                hold(sp, "sp", gps.handle, gps.at(g, blk - 2, 1))
                sp.dma_start(h1[:, p, :], h1_d[bass.ds(n8, 1)].rearrange("o p n -> (o p) n")
                             ).then_inc(h1_in[p], 16)

            with sp.Fori(0, GROUPS) as g:
                for blk in range(UN):
                    load_block(g, blk, False)

            hold(sp, "sp", oacc.handle, oacc.at(GROUPS - 1, UN - 1, 4))
            sp.dma_start(fw[:], fw_d.rearrange("(a p) d -> p a d", p=P)).then_inc(f_in, 16)
            sp.dma_start(fb[:], fb_d.rearrange("(a d) -> a d", a=1).broadcast_to([P, HID])).then_inc(f_in, 16)
            with sp.Fori(0, BLOCKS) as i:
                hold(sp, "sp", f_out, i * C + C)
                sp.dma_start(out_d[bass.ds(i * NT, NT), :].rearrange("(c p) d -> p c d", p=P),
                             xa[:, bass.ds(i * C, C), :]).then_inc(f_st, 16)
            hold(sp, "sp", f_st, BLOCKS * 16)

        @block.tensor
        def _(pe):
            mm = nc.tensor.matmul
            tr = nc.tensor.transpose

            pe.wait_ge(const_in, 16 * 9)
            with pe.Fori(0, BLOCKS) as i:
                pe.wait_ge(pr_h, i * C + C)
                pe.wait_ge(pr_hT, i * 2)
                for k in range(KT):
                    for c in range(C):
                        t = tr(Z[k][:, c * P:(c + 1) * P], hn[:, c, k * P:(k + 1) * P], eye[:])
                    t.then_inc(pr_tr, 1)
                pe.wait_ge(pr_hT, i * 2 + 2)
                for j, w in enumerate((wf1, wg1)):
                    if j == 0:
                        pe.wait_ge(pr_lowc, i * 2)
                    for k in range(KT):
                        t = mm(X[j][:], lhsT=w[:, k, :], rhs=hTb[:, k, :], start=k == 0, stop=k == KT - 1)
                    t.then_inc(pr_low, 1)
                pe.wait_ge(pr_betac, i)
                for c in range(C):
                    for k in range(KT):
                        t = mm(O[:, c * H:(c + 1) * H], lhsT=hTb[:, k, c * P:(c + 1) * P], rhs=wb[:, k, :],
                               start=k == 0, stop=k == KT - 1)
                t.then_inc(pr_beta, 1)
                pe.wait_ge(pr_lowc, i * 2 + 1)
                for c in range(C):
                    for j in range(4):
                        q = c * 4 + j
                        if q < 2:
                            pe.wait_ge(pr_zc, i * 16)
                        else:
                            pe.wait_ge(pr_zc, i * 16 + q - 1)
                        mm(L[q % 2][:], lhsT=low[:, 0, c * P:(c + 1) * P], rhs=wf2[:, j * 512:(j + 1) * 512],
                           start=True, stop=True).then_inc(pr_z, 1)
            pe.wait_ge(pr_bset, 1)

            def project(g, blk, i):
                if i == 0:
                    if blk % UN == 0:
                        pe.wait_ge(w_in, g * 32 + (blk // UN) * 32 + 32)
                    pe.wait_ge(ht_in[par(blk)], loads(g, blk))
                if i < 2:
                    pe.wait_ge(aevac.handle, aevac.at(g, blk - 1, 3 + i))
                else:
                    pe.wait_ge(pevac.handle, pevac.at(g, blk, 2 * (i - 2) + 2))
                for k in range(KT):
                    t = mm(X[i % 2][:], lhsT=wh[:, k, i, :], rhs=hT[:, par(blk), k, :],
                           start=k == 0, stop=k == KT - 1)
                t.then_inc(proj.handle, 1)

            def w_norms(g, blk):
                pe.wait_ge(wsq.handle, wsq.at(g, blk, 1))
                pe.wait_ge(rsv.handle, rsv.at(g, blk - 1, 2))
                for c in range(C):
                    t = mm(S[:, 256 + c:257 + c], lhsT=ysq[:, c * P:(c + 1) * P], rhs=ones[:], start=True, stop=True)
                t.then_inc(wss.handle, 1)
                pe.wait_ge(cnat.handle, cnat.at(g, blk, 1))
                for q in range(2):
                    t = mm(S[:, 260 + q * C:260 + (q + 1) * C], lhsT=perm[:, q, :], rhs=cc[:, 2, :],
                           start=True, stop=True)
                t.then_inc(cperm.handle, 1)

            def step_sums(g, blk):
                pe.wait_ge(g_in[par(blk)], loads(g, blk))
                for c in range(C):
                    w = gl[:, par(blk), c * P:(c + 1) * P]
                    if c == 0:
                        pe.wait_ge(oacc.handle, oacc.at(g, blk - 1, 4))
                    else:
                        pe.wait_ge(expA.handle, expA.at(g, blk, 2 * c))
                    mm(L[0][:], lhsT=w, rhs=msum[:, 0:512], start=True, stop=True).then_inc(lsum.handle, 1)
                    if c > 0:
                        pe.wait_ge(expB.handle, expB.at(g, blk, c))
                    mm(L[1][:, 0:384], lhsT=w, rhs=msum[:, 512:896], start=True, stop=True
                       ).then_inc(lsum.handle, 1)

            def qk_products(g, blk):
                pe.wait_ge(packs.handle, packs.at(g, blk, 8))
                for c in range(C):
                    if c < 2:
                        pe.wait_ge(pevac.handle, pevac.at(g, blk, 2 * (c + 2) + 2))
                    else:
                        pe.wait_ge(aevac.handle, aevac.at(g, blk, c - 1))
                    for q in range(2):
                        mm(X[c % 2][:, q * P:(q + 1) * P], lhsT=pk[:, 0, c, q * P:(q + 1) * P],
                           rhs=pk[:, 1, c, q * P:(q + 1) * P], start=True, stop=True)
                    mm(X[c % 2][:, 256:384], lhsT=y[:, 1, c * P:(c + 1) * P], rhs=y[:, 0, c * P:(c + 1) * P],
                       start=True, stop=True).then_inc(qk.handle, 1)

            def u_transposes(g, blk):
                for c in range(C):
                    if c == 0:
                        pe.wait_ge(wprod.handle, wprod.at(g, blk, 6))
                        pe.wait_ge(sexp.handle, sexp.at(g, blk - 1, 4))
                    elif c == 1:
                        pe.wait_ge(aes.handle, aes.at(g, blk - 1, 5))
                    else:
                        pe.wait_ge(uevac.handle, uevac.at(g, blk, 2 * (c - 1)))
                    for q in range(4):
                        t = tr(Z[c % 2][:, q * P:(q + 1) * P], EL[:, c, q * P:(q + 1) * P], eye[:])
                    t.then_inc(utr.handle, 1)

            def kv_transposes(g, blk):
                pe.wait_ge(packs.handle, packs.at(g, blk, 12))
                for c in range(C):
                    if c < 2:
                        pe.wait_ge(uevac.handle, uevac.at(g, blk, 2 * (c + 3)))
                    else:
                        pe.wait_ge(kvevac.handle, kvevac.at(g, blk, c - 1))
                    tr(Z[c % 2][:, 0:P], y[:, 1, c * P:(c + 1) * P], eye[:])
                    tr(Z[c % 2][:, P:2 * P], y[:, 2, c * P:(c + 1) * P], eye[:])
                    tr(Z[c % 2][:, 2 * P:3 * P], pk[:, 2, c, 0:P], eye[:])
                    tr(Z[c % 2][:, 3 * P:4 * P], pk[:, 2, c, P:2 * P], eye[:]).then_inc(kvtr.handle, 1)

            def states(g, blk):
                pe.wait_ge(call.handle, call.at(g, blk, 1))
                for c in range(C):
                    pe.wait_ge(uevac.handle, uevac.at(g, blk, 2 * c + 2))
                    pe.wait_ge(kvevac.handle, kvevac.at(g, blk, c + 1))
                    pe.wait_ge(stupd.handle, stupd.at(g, blk, c))
                    mm(S[:, 0:256], lhsT=U[:, c, 0:P], rhs=kv[:, c, 0:256], start=True, stop=True
                       ).then_inc(stps.handle, 1)
                pe.wait_ge(kvevac.handle, kvevac.at(g, blk, 3))
                pe.wait_ge(stupd.handle, stupd.at(g, blk, 3))
                for c in range(C):
                    t = tr(Z[0][:, c * P:(c + 1) * P], ST[:, c, 0:P], eye[:])
                t.then_inc(sktr.handle, 1)

            def scores(g, blk):
                pe.wait_ge(skevac.handle, skevac.at(g, blk, 1))
                for c in range(C):
                    pe.wait_ge(aevac.handle, aevac.at(g, blk, c + 1))
                    if c == 0:
                        pe.wait_ge(expA.handle, expA.at(g, blk, 8))
                    elif c == 1:
                        pe.wait_ge(expB.handle, expB.at(g, blk, 4))
                    else:
                        pe.wait_ge(prods.handle, prods.at(g, blk, c - 1))
                    mm(L[c % 2][:, 0:P], lhsT=Sk[:, c, :], rhs=y[:, 0, c * P:(c + 1) * P], start=True, stop=True)
                    mm(L[c % 2][:, P:2 * P], lhsT=U[:, c, DNEG:DNEG + P], rhs=A[:, c, 256:384],
                       start=True, stop=True)
                    for q in range(2):
                        t = mm(L[c % 2][:, (2 + q) * P:(3 + q) * P], lhsT=U[:, c, (1 + q) * P:(2 + q) * P],
                               rhs=A[:, c, q * P:(q + 1) * P], start=True, stop=True)
                    t.then_inc(sc.handle, 1)

            def score_transposes(g, blk):
                pe.wait_ge(adds.handle, adds.at(g, blk, 5))
                for c in range(C):
                    t = tr(Z[0][:, c * P:(c + 1) * P], pr[:, c, 0:P], eye[:])
                t.then_inc(strn.handle, 1)

            def gate_product(g, blk):
                if blk == 0:
                    pe.wait_ge(w2_in, g * 48 + 48)
                pe.wait_ge(h1_in[par(blk)], loads(g, blk))
                pe.wait_ge(prods.handle, prods.at(g, blk, 3))
                mm(L[0][:], lhsT=wg2[:], rhs=h1[:, par(blk), :], start=True, stop=True).then_inc(gps.handle, 1)

            def a_transposes(g, blk):
                pe.wait_ge(sexp.handle, sexp.at(g, blk, 4))
                for c in range(C):
                    t = tr(Z[1][:, c * P:(c + 1) * P], a[:, c, :], eye[:])
                t.then_inc(atrn.handle, 1)

            def p_products(g, blk):
                pe.wait_ge(aes.handle, aes.at(g, blk, 5))
                for c in range(C):
                    if c == 0:
                        pe.wait_ge(prods.handle, prods.at(g, blk, 4))
                    elif c == 1:
                        pe.wait_ge(gth.handle, gth.at(g, blk, 1))
                    else:
                        pe.wait_ge(pevc.handle, pevc.at(g, blk, c - 1))
                    b = L[(c + 1) % 2]
                    for q in range(2):
                        mm(b[:, q * P:(q + 1) * P], lhsT=EL[:, c, (1 + q) * P:(2 + q) * P],
                           rhs=AE[:, c, (2 + q) * P:(3 + q) * P], start=True, stop=True)
                    mm(b[:, 256:384], lhsT=EL[:, c, DNEG:DNEG + P], rhs=AE[:, c, DPOS:DPOS + P],
                       start=True, stop=True).then_inc(pps.handle, 1)

            def o_products(g, blk):
                for c in range(C):
                    oc = O[:, c * P:(c + 1) * P]
                    mm(oc, lhsT=ST[:, c, P:2 * P], rhs=AE[:, c, INCL:INCL + P], start=True, stop=False)
                    pe.wait_ge(pevc.handle, pevc.at(g, blk, c + 1))
                    mm(oc, lhsT=kv[:, c, P:2 * P], rhs=Pm[:, c, 256:384], start=False, stop=False)
                    for v, s in enumerate(LEVELS):
                        orr = oc.rearrange("p (n two s) -> p n two s", two=2, s=s)[:, :, 1, :]
                        t = mm(orr, lhsT=kv[:, c, (2 + v // 2) * P:(3 + v // 2) * P],
                               rhs=Pm[:, c, v * 64:(v + 1) * 64].rearrange("p (n s) -> p n s", s=s),
                               start=False, stop=v == 3)
                t.then_inc(ops.handle, 1)

            def out_products(g, blk):
                pe.wait_ge(osqs.handle, osqs.at(g, blk, 1))
                for c in range(C):
                    t = mm(S[:, 268 + c:269 + c], lhsT=osq[:, c * P:(c + 1) * P], rhs=ones[:], start=True, stop=True)
                t.then_inc(rss.handle, 1)
                pe.wait_ge(ogs.handle, ogs.at(g, blk, 1))
                if blk == 0:
                    pe.wait_ge(wos_set, g + 1)
                for j in range(2):
                    pe.wait_ge(pevc.handle, pevc.at(g, blk, 3 + j))
                    for c in range(2):
                        t = mm(L[(j + 1) % 2][:, c * HID:(c + 1) * HID],
                               lhsT=og[:, (2 * j + c) * P:(2 * j + c + 1) * P], rhs=wos[:], start=True, stop=True)
                    t.then_inc(wops.handle, 1)

            def front_b(g, blk):
                step_sums(g, blk)
                qk_products(g, blk)
                u_transposes(g, blk)
                kv_transposes(g, blk)
                states(g, blk)
                scores(g, blk)

            def first():
                for i in range(4):
                    project(0, 0, i)
                w_norms(0, 0)
                front_b(0, 0)

            def slot(g, blk, more):
                score_transposes(g, blk)
                gate_product(g, blk)
                if more:
                    project(g, blk + 1, 0)
                a_transposes(g, blk)
                if more:
                    project(g, blk + 1, 1)
                    project(g, blk + 1, 2)
                p_products(g, blk)
                if more:
                    project(g, blk + 1, 3)
                o_products(g, blk)
                out_products(g, blk)
                if more:
                    w_norms(g, blk + 1)
                    front_b(g, blk + 1)

            run(pe, slot, first)

            pe.wait_ge(f_wq, 1)
            zb = [Z[0][:].bitcast(BF16), Z[1][:].bitcast(BF16)]
            for k in range(KT):
                for o in range(KT):
                    t = tr(zb[0][:, (k * 2 + o) * P:(k * 2 + o + 1) * P], fwq[:, o, k * P:(k + 1) * P], eyeb[:])
            t.then_inc(f_tr, 1)
            pe.wait_ge(f_trc, 1)
            with pe.Fori(0, BLOCKS) as i:
                pe.wait_ge(f_q, i + 1)
                for c in range(C):
                    pe.wait_ge(f_out, i * C)
                    for k in range(KT):
                        t = tr(zb[1][:, (c * 2 + k) * P:(c * 2 + k + 1) * P],
                               fq[:, bass.ds(i * C + c, 1), k * P:(k + 1) * P].rearrange("p o n -> p (o n)"),
                               eyeb[:])
                t.then_inc(f_tr, 1)
                pe.wait_ge(f_trc, i + 2)
                for c in range(C):
                    for k in range(KT):
                        t = mm(X[c // 2][:, (c % 2) * HID:(c % 2 + 1) * HID], lhsT=fqT[:, c, k, :],
                               rhs=fwT[:, k, :], start=k == 0, stop=k == KT - 1)
                t.then_inc(f_mm, 1)

        @block.scalar
        def _(act):
            fn = nc.scalar.activation
            with act.Fori(0, BLOCKS) as i:
                act.wait_ge(pr_sg, i * 128)
                for q in range(16):
                    c, j = q // 4, q % 4
                    act.wait_ge(pr_zc, i * 16 + q + 1)
                    zz = zs[:, c, j * 512:(j + 1) * 512]
                    fn(zz, zz, ACT.Exp, scale=-1.0).then_inc(pr_exp, 1)
                for q in range(16):
                    c, j = q // 4, q % 4
                    act.wait_ge(pr_exp, i * 16 + q + 1)
                    zz = zs[:, c, j * 512:(j + 1) * 512]
                    fn(zz, zz, ACT.Ln, bias=1.0).then_inc(pr_ln, 1)
            act.wait_ge(pr_betac, BLOCKS)
            fn(beta[:], braw[:], ACT.Tanh, scale=0.5).then_inc(pr_tanh, 1)
            act.wait_ge(pr_bset, 1)
            for s_ in (halo, pevac, tanh, wsq, expA, expB, uevac, kvevac, skevac, sexp, gth, osqs):
                act.sem_inc(s_.handle, 2 * s_.per)

            def evacuate(g, blk, i):
                act.wait_ge(conv.handle, conv.at(g, blk - 1, 3 * i + 3))
                if blk % UN == 0:
                    nc.scalar.activation(xb[:, i, 1:4], eye[:, 0:3], ACT.Copy, scale=0.0).then_inc(halo.handle, 1)
                else:
                    nc.scalar.copy(xb[:, i, 1:4], xb[:, i, NT + 1:NT + 4]).then_inc(halo.handle, 1)
                if i == 0:
                    act.wait_ge(sc.handle, sc.at(g, blk - 1, 4))
                act.wait_ge(proj.handle, proj.at(g, blk, i + 1))
                act.wait_ge(halo.handle, halo.at(g, blk, i + 1))
                fn(xb[:, i, 4:NT + 4], X[i % 2][:], ACT.Copy).then_inc(pevac.handle, 1)
                fn(y[:, i, :], X[i % 2][:], ACT.Copy, scale=cw[:, i, 3:4]).then_inc(pevac.handle, 1)

            def half_tanh(g, blk, i):
                act.wait_ge(conv.handle, conv.at(g, blk, 3 * i + 3))
                act.wait_ge(silu.handle, silu.at(g, blk - 1, i + 3))
                fn(th[:, i % 2, :], y[:, i, :], ACT.Tanh, scale=0.5).then_inc(tanh.handle, 1)

            def w_square(g, blk):
                act.wait_ge(silu.handle, silu.at(g, blk, 4))
                fn(ysq[:], y[:, 3, :], ACT.Square).then_inc(wsq.handle, 1)

            def decays(g, blk):
                act.wait_ge(aes.handle, aes.at(g, blk - 1, 5))
                act.wait_ge(pps.handle, pps.at(g, blk - 1, 4))
                for c in range(C):
                    act.wait_ge(lsum.handle, lsum.at(g, blk, 2 * c + 1))
                    fn(ER[:, c, :], L[0][:], ACT.Exp, scale=-1.0).then_inc(expA.handle, 1)
                    fn(EL[:, c, DNEG:DNEG + P], L[0][:, DPOS:DPOS + P], ACT.Exp).then_inc(expA.handle, 1)
                    act.wait_ge(lsum.handle, lsum.at(g, blk, 2 * c + 2))
                    fn(EL[:, c, 0:384], L[1][:, 0:384], ACT.Exp, scale=-1.0).then_inc(expB.handle, 1)

            def u_copies(g, blk):
                act.wait_ge(call.handle, call.at(g, blk, 1))
                for c in range(C):
                    act.wait_ge(utr.handle, utr.at(g, blk, c + 1))
                    fn(U[:, c, 0:P], Z[c % 2][:, 0:P], ACT.Copy, scale=cc[:, 2, c:c + 1]).then_inc(uevac.handle, 1)
                    fn(U[:, c, P:512], Z[c % 2][:, P:512], ACT.Copy).then_inc(uevac.handle, 1)

            def kv_copies(g, blk):
                for c in range(C):
                    act.wait_ge(kvtr.handle, kvtr.at(g, blk, c + 1))
                    fn(kv[:, c, :], Z[c % 2][:], ACT.Copy).then_inc(kvevac.handle, 1)

            def state_copy(g, blk):
                act.wait_ge(sktr.handle, sktr.at(g, blk, 1))
                fn(Sk[:].rearrange("p c m -> p (c m)"), Z[0][:], ACT.Copy).then_inc(skevac.handle, 1)

            def softmax(g, blk):
                act.wait_ge(nmax.handle, nmax.at(g, blk, 1))
                for c in range(C):
                    fn(a[:, c, :], Z[0][:, c * P:(c + 1) * P], ACT.Exp, bias=nm[:, c:c + 1], scale=SC,
                       accum_out=den[:, c:c + 1]).then_inc(sexp.handle, 1)

            def gate(g, blk):
                if blk == 0:
                    act.wait_ge(wos_set, g + 1)
                act.wait_ge(ogs.handle, ogs.at(g, blk - 1, 1))
                act.wait_ge(gps.handle, gps.at(g, blk, 1))
                fn(gt[:], L[0][:], ACT.Tanh, bias=bgh[:, 0:1], scale=0.5).then_inc(gth.handle, 1)

            def o_square(g, blk):
                act.wait_ge(ogs.handle, ogs.at(g, blk, 1))
                fn(osq[:], O[:], ACT.Square).then_inc(osqs.handle, 1)

            def front_b(g, blk):
                decays(g, blk)
                u_copies(g, blk)
                kv_copies(g, blk)
                state_copy(g, blk)

            def first():
                for i in range(4):
                    evacuate(0, 0, i)
                    if i > 0:
                        half_tanh(0, 0, i - 1)
                half_tanh(0, 0, 3)
                w_square(0, 0)
                front_b(0, 0)

            def slot(g, blk, more):
                softmax(g, blk)
                gate(g, blk)
                if more:
                    evacuate(g, blk + 1, 0)
                    evacuate(g, blk + 1, 1)
                    half_tanh(g, blk + 1, 0)
                    evacuate(g, blk + 1, 2)
                    half_tanh(g, blk + 1, 1)
                    evacuate(g, blk + 1, 3)
                    half_tanh(g, blk + 1, 2)
                    half_tanh(g, blk + 1, 3)
                    w_square(g, blk + 1)
                o_square(g, blk)
                if more:
                    front_b(g, blk + 1)

            run(act, slot, first)

            act.wait_ge(f_tr, 1)
            fn(fwT[:].rearrange("p k n -> p (k n)"), Z[0][:].bitcast(BF16)[:, 0:512], ACT.Copy).then_inc(f_trc, 1)
            with act.Fori(0, BLOCKS) as i:
                act.wait_ge(f_tr, i + 2)
                fn(fqT[:].rearrange("p c k n -> p (c k n)"), Z[1][:].bitcast(BF16), ACT.Copy).then_inc(f_trc, 1)

        @block.vector
        def _(dve):
            v = nc.vector
            TT, TS, STT = v.tensor_tensor, v.tensor_scalar, v.scalar_tensor_tensor

            v.memset(ones[:], 1.0)
            v.memset(half[:], -0.5).then_inc(ones_set, 1)
            dve.wait_ge(const_in, 16 * 9)
            TS(nwh[:], nw[:], 0.5, None, ALU.mult).then_inc(ones_set, 1)
            v.tensor_copy(eyeb[:], eye[:]).then_inc(ones_set, 1)
            with dve.Fori(0, BLOCKS) as i:
                dve.wait_ge(x_in, i * 16 + 16)
                for c in range(C):
                    v.bn_stats(stat[:, c, :], xa[:, bass.ds(i * C + c, 1), :].rearrange("p o d -> p (o d)")
                               ).then_inc(pr_stat, 1)
                for c in range(C):
                    hold(dve, "dve", pr_stat, i * C + c + 1)
                    v.bn_aggr(mv[:, c, :], stat[:, c, :]).then_inc(pr_aggr, 1)
                dve.wait_ge(pr_aggr, i * C + C)
                TS(var[:], mv[:, :, 1], EPS, None, ALU.add).then_inc(pr_var, 1)
                dve.wait_ge(pr_rstd, i + 1)
                dve.wait_ge(pr_tr, i * 2)
                for c in range(C):
                    TS(hn[:, c, :], xa[:, bass.ds(i * C + c, 1), :].rearrange("p o d -> p (o d)"),
                       mv[:, c, 0:1], rstd[:, c:c + 1], ALU.subtract, ALU.mult).then_inc(pr_h, 1)
                dve.wait_ge(pr_st, i * 32)
                dve.wait_ge(pr_beta, i)
                dve.wait_ge(pr_z, i * 16)
                for k in range(KT):
                    dve.wait_ge(pr_tr, i * 2 + k + 1)
                    v.tensor_copy(hTb[:, k, :], Z[k][:]).then_inc(pr_hT, 1)
                for j in range(2):
                    dve.wait_ge(pr_low, i * 2 + j + 1)
                    v.tensor_copy(low[:, j, :], X[j][:]).then_inc(pr_lowc, 1)
                dve.wait_ge(pr_beta, i + 1)
                v.tensor_copy(braw[:, :, bass.ds(i * C, C)],
                              O[:, 0:C * H].rearrange("p (c h) -> p h c", h=H)).then_inc(pr_betac, 1)
                dve.wait_ge(pr_sg, i * 128)
                for q in range(16):
                    c, j = q // 4, q % 4
                    dve.wait_ge(pr_z, i * 16 + q + 1)
                    TS(zs[:, c, j * 512:(j + 1) * 512], L[q % 2][:], ZMIN, None, ALU.max).then_inc(pr_zc, 1)
            dve.wait_ge(pr_tanh, 1)
            dve.wait_ge(pr_sg, BLOCKS * 128)
            dve.wait_ge(pr_st, BLOCKS * 32)
            TS(beta[:], beta[:], 1.0, 0.5, ALU.add, ALU.mult).then_inc(pr_bset, 1)
            dve.wait_ge(pr_bset, 1)
            for s_ in (conv, silu, cv, cnat, call, wprod, st0, stupd, aevac, prods, adds, smax, nmax, aes,
                       pevc, ogs, rsv, oacc):
                dve.sem_inc(s_.handle, 2 * s_.per)

            def taps(g, blk, i):
                for j in range(3):
                    if j == 0:
                        dve.wait_ge(pevac.handle, pevac.at(g, blk, 2 * i + 2))
                    else:
                        dve.wait_ge(conv.handle, conv.at(g, blk, 3 * i + j))
                    STT(out=y[:, i, :], in0=xb[:, i, 1 + j:1 + j + NT], scalar=cw[:, i, j:j + 1], in1=y[:, i, :],
                        op0=ALU.mult, op1=ALU.add).then_inc(conv.handle, 1)

            def twice_silu(g, blk, i):
                dve.wait_ge(tanh.handle, tanh.at(g, blk, i + 1))
                STT(out=y[:, i, :], in0=th[:, i % 2, :], scalar=1.0, in1=y[:, i, :], op0=ALU.add, op1=ALU.mult
                    ).then_inc(silu.handle, 1)

            def w_factor(g, blk):
                dve.wait_ge(wss.handle, wss.at(g, blk, 1))
                TS(cvv[:], S[:, 256:260], 4.0 * L2EPS, None, ALU.add).then_inc(cv.handle, 1)
                dve.wait_ge(cpow.handle, cpow.at(g, blk, 1))
                dve.wait_ge(mcs.handle, mcs.at(g, blk - 1, 1))
                h_at = g * (UN * C) + blk * C
                TT(cc[:, 2, :], cpw[:], beta[:].rearrange("p h c -> p (h c)")[:, bass.ds(h_at, C)], ALU.mult
                   ).then_inc(cnat.handle, 1)
                dve.wait_ge(cperm.handle, cperm.at(g, blk, 1))
                v.tensor_copy(cc[:, 0:2, :].rearrange("p q c -> p (q c)"), S[:, 260:268]).then_inc(call.handle, 1)
                dve.wait_ge(cnat.handle, cnat.at(g, blk, 1))
                dve.sem_inc(call.handle, 1)

            def w_products(g, blk):
                dve.wait_ge(expA.handle, expA.at(g, blk, 8))
                dve.wait_ge(expB.handle, expB.at(g, blk, 4))
                yw = y[:, 3, :]
                ywc = yw.rearrange("p (c m) -> p c m", c=C)
                TT(EL[:, :, SUF:SUF + P], ywc, EL[:, :, SUF:SUF + P], ALU.mult).then_inc(wprod.handle, 1)
                for q, s in enumerate(LEVELS):
                    e = packed(EL, LEFT + 64 * q, s)
                    TT(e, left(yw, s), e, ALU.mult).then_inc(wprod.handle, 1)
                TT(EL[:, :, DNEG:DNEG + P], ywc, EL[:, :, DNEG:DNEG + P], ALU.mult).then_inc(wprod.handle, 1)

            def a_masks(g, blk):
                dve.wait_ge(mcs.handle, mcs.at(g, blk, 1))
                for c in range(C):
                    dve.wait_ge(qk.handle, qk.at(g, blk, c + 1))
                    TT(A[:, c, :], X[c % 2][:, 0:384], mc[:, c, :], ALU.mult).then_inc(aevac.handle, 1)

            def start_state(g, blk):
                dve.wait_ge(ops.handle, ops.at(g, blk - 1, 1))
                if blk % UN == 0:
                    v.memset(ST[:, 0, :], 0.0).then_inc(st0.handle, 1)
                else:
                    dve.wait_ge(stupd.handle, stupd.at(g, blk - 1, 4))
                    v.tensor_copy(ST[:, 0, :], ST[:, C, :]).then_inc(st0.handle, 1)

            def state_updates(g, blk):
                dve.wait_ge(st0.handle, st0.at(g, blk, 1))
                for c in range(C):
                    dve.wait_ge(stps.handle, stps.at(g, blk, c + 1))
                    if c > 0:
                        dve.wait_ge(stupd.handle, stupd.at(g, blk, c))
                    STT(out=ST[:, c + 1, :], in0=ST[:, c, :], scalar=ER[:, c, P - 1:P], in1=S[:, 0:256],
                        op0=ALU.mult, op1=ALU.add).then_inc(stupd.handle, 1)

            def score_products(g, blk):
                for c in range(C):
                    dve.wait_ge(sc.handle, sc.at(g, blk, c + 1))
                    TT(pr[:, c, :], L[c % 2][:], ER[:, c, :], ALU.mult).then_inc(prods.handle, 1)
                dve.wait_ge(prods.handle, prods.at(g, blk, 4))
                s_all = pr[:, :, 0:P]
                TT(s_all, s_all, pr[:, :, DPOS:DPOS + P], ALU.add).then_inc(adds.handle, 1)
                for q, s in enumerate(LEVELS):
                    dve.wait_ge(adds.handle, adds.at(g, blk, q + 1))
                    dst = s_all.rearrange("p c (n two s) -> p c n two s", two=2, s=s)[:, :, :, 1, :]
                    TT(dst, dst, packed(pr, RIGHT + 64 * q, s), ALU.add).then_inc(adds.handle, 1)

            def row_max(g, blk):
                dve.wait_ge(strn.handle, strn.at(g, blk, 1))
                v.tensor_reduce(out=mx[:], in_=Z[0][:].rearrange("p (c m) -> p c m", c=C), axis=AX.X, op=ALU.max
                                ).then_inc(smax.handle, 1)
                dve.wait_ge(smax.handle, smax.at(g, blk, 1))
                TS(nm[:], mx[:], -SC, None, ALU.mult).then_inc(nmax.handle, 1)

            def a_decays(g, blk):
                dve.wait_ge(atrn.handle, atrn.at(g, blk, 1))
                at = Z[1][:]
                TT(AE[:, :, 0:256].rearrange("p c (w m) -> p c w m", w=2),
                   at.rearrange("p (c m) -> p c m", c=C).unsqueeze(2).broadcast_to([P, C, 2, P]),
                   ER[:, :, 0:256].rearrange("p c (w m) -> p c w m", w=2), ALU.mult).then_inc(aes.handle, 1)
                for q, s in enumerate(LEVELS):
                    TT(packed(AE, RIGHT + 64 * q, s), right(at, s), packed(ER, RIGHT + 64 * q, s), ALU.mult
                       ).then_inc(aes.handle, 1)

            def p_masks(g, blk):
                for c in range(C):
                    dve.wait_ge(pps.handle, pps.at(g, blk, c + 1))
                    TT(Pm[:, c, :], L[(c + 1) % 2][:, 0:384], mc[:, c, :], ALU.mult).then_inc(pevc.handle, 1)

            def o_gate(g, blk):
                dve.wait_ge(ops.handle, ops.at(g, blk, 1))
                dve.wait_ge(gth.handle, gth.at(g, blk, 1))
                STT(out=og[:], in0=gt[:], scalar=1.0, in1=O[:], op0=ALU.add, op1=ALU.mult).then_inc(ogs.handle, 1)

            def o_add(g, blk):
                dve.wait_ge(sexp.handle, sexp.at(g, blk, 4))
                STT(out=r0[:], in0=den[:], scalar=4.0 * EPS, in1=den[:], op0=ALU.mult, op1=ALU.mult
                    ).then_inc(rsv.handle, 1)
                dve.wait_ge(rss.handle, rss.at(g, blk, 1))
                dve.wait_ge(rsv.handle, rsv.at(g, blk, 1))
                STT(out=r1[:], in0=S[:, 268:272], scalar=1.0 / P, in1=r0[:], op0=ALU.mult, op1=ALU.add
                    ).then_inc(rsv.handle, 1)
                dve.wait_ge(rpow.handle, rpow.at(g, blk, 1))
                for c in range(C):
                    if c % 2 == 0:
                        dve.wait_ge(wops.handle, wops.at(g, blk, c // 2 + 1))
                    xc = xa[:, bass.ds((g % 2) * (UN * C) + (blk * C + c), 1), :].rearrange("p o d -> p (o d)")
                    STT(out=xc, in0=L[(c // 2 + 1) % 2][:, (c % 2) * HID:(c % 2 + 1) * HID], scalar=rr[:, c:c + 1],
                        in1=xc, op0=ALU.mult, op1=ALU.add).then_inc(oacc.handle, 1)

            def front_b(g, blk):
                start_state(g, blk)
                w_products(g, blk)
                a_masks(g, blk)
                state_updates(g, blk)
                score_products(g, blk)

            def first():
                for i in range(4):
                    taps(0, 0, i)
                    twice_silu(0, 0, i)
                w_factor(0, 0)
                front_b(0, 0)

            def slot(g, blk, more):
                row_max(g, blk)
                if more:
                    taps(g, blk + 1, 0)
                    twice_silu(g, blk + 1, 0)
                a_decays(g, blk)
                if more:
                    taps(g, blk + 1, 1)
                    twice_silu(g, blk + 1, 1)
                p_masks(g, blk)
                if more:
                    taps(g, blk + 1, 2)
                    taps(g, blk + 1, 3)
                    twice_silu(g, blk + 1, 2)
                    twice_silu(g, blk + 1, 3)
                o_gate(g, blk)
                o_add(g, blk)
                if more:
                    w_factor(g, blk + 1)
                    front_b(g, blk + 1)

            run(dve, slot, first)

            dve.wait_ge(oacc.handle, oacc.at(GROUPS - 1, UN - 1, 4))
            with dve.Fori(0, BLOCKS) as i:
                for c in range(C):
                    v.bn_stats(fstat[:, c, :], xa[:, bass.ds(i * C + c, 1), :].rearrange("p o d -> p (o d)")
                               ).then_inc(f_stat, 1)
                for c in range(C):
                    hold(dve, "dve", f_stat, i * C + c + 1)
                    v.bn_aggr(fmv[:, c, :], fstat[:, c, :]).then_inc(f_aggr, 1)
                dve.wait_ge(f_aggr, i * C + C)
                TS(fvar[:], fmv[:, :, 1], EPS, None, ALU.add).then_inc(f_var, 1)
                dve.wait_ge(f_rstd, i + 1)
                for c in range(C):
                    TS(fy[:, bass.ds(i * C + c, 1), :].rearrange("p o d -> p (o d)"),
                       xa[:, bass.ds(i * C + c, 1), :].rearrange("p o d -> p (o d)"),
                       fmv[:, c, 0:1], frstd[:, c:c + 1], ALU.subtract, ALU.mult).then_inc(f_y, 1)
                dve.wait_ge(f_y, i * C + C)
                yblk = fy[:, bass.ds(i * C, C), :].rearrange("p c d -> p (c d)")
                v.tensor_reduce(out=fhi[:, bass.ds(i, 1)], in_=yblk, axis=AX.X, op=ALU.max).then_inc(f_mx, 1)
                v.tensor_reduce(out=flo[:, bass.ds(i, 1)], in_=yblk, axis=AX.X, op=ALU.min).then_inc(f_mx, 1)
            dve.wait_ge(f_in, 32)
            fwf = fw[:].rearrange("p a d -> p (a d)")
            v.tensor_reduce(out=fs[:, 0:1], in_=fwf, axis=AX.X, op=ALU.max).then_inc(f_wmx, 1)
            v.tensor_reduce(out=fs[:, 1:2], in_=fwf, axis=AX.X, op=ALU.min).then_inc(f_wmx, 1)
            dve.wait_ge(f_mx, 2 * BLOCKS)
            v.tensor_reduce(out=fs[:, 2:3], in_=fhi[:], axis=AX.X, op=ALU.max).then_inc(f_wmx, 1)
            v.tensor_reduce(out=fs[:, 3:4], in_=flo[:], axis=AX.X, op=ALU.min).then_inc(f_wmx, 1)
            dve.wait_ge(f_wmx, 4)
            STT(out=fs[:, 4:5], in0=fs[:, 3:4], scalar=-1.0, in1=fs[:, 2:3], op0=ALU.mult, op1=ALU.max
                ).then_inc(f_amax, 1)
            STT(out=fs[:, 5:6], in0=fs[:, 1:2], scalar=-1.0, in1=fs[:, 0:1], op0=ALU.mult, op1=ALU.max
                ).then_inc(f_amax, 1)
            dve.wait_ge(f_all, 1)
            TT(fs[:, 7:8], fs[:, 7:8], fs[:, 6:7], ALU.max).then_inc(f_sc, 1)
            dve.wait_ge(f_sc, 1)
            TS(fs[:, 8:10], fs[:, 6:8], 1.0 / QMAX, None, ALU.mult).then_inc(f_sc, 1)
            dve.wait_ge(f_sc, 2)
            v.reciprocal(fs[:, 10:12], fs[:, 8:10]).then_inc(f_sc, 1)
            TT(fs[:, 12:13], fs[:, 8:9], fs[:, 9:10], ALU.mult).then_inc(f_sc, 1)
            dve.wait_ge(f_sc, 4)

            quant_count = [0]

            def to_fp8(dst, src, inv, n, done, base):
                TS(fu[:, 0:n], src, inv, None, ALU.mult).then_inc(f_xb, 1)
                dve.wait_ge(f_xb, base + 1)
                TS(fm[:, 0:n].bitcast(U32), fu[:, 0:n].bitcast(U32), 0x7F800000, None, ALU.bitwise_and
                   ).then_inc(f_xb, 1)
                dve.wait_ge(f_xb, base + 2)
                TS(fm[:, 0:n], fm[:, 0:n], 2.0 ** -6, 1.5 * 2.0 ** 20, ALU.max, ALU.mult).then_inc(f_xb, 1)
                dve.wait_ge(f_xb, base + 3)
                TT(fu[:, 0:n], fu[:, 0:n], fm[:, 0:n], ALU.add).then_inc(f_xb, 1)
                dve.wait_ge(f_xb, base + 4)
                TT(dst, fu[:, 0:n], fm[:, 0:n], ALU.subtract).then_inc(done, 1)

            to_fp8(fwq[:].rearrange("p a d -> p (a d)"), fwf, fs[:, 11:12], KT * HID, f_wq, 0)
            dve.wait_ge(f_wq, 1)
            with dve.Fori(0, BLOCKS) as i:
                to_fp8(fq[:, bass.ds(i * C, C), :].rearrange("p c d -> p (c d)"),
                       fy[:, bass.ds(i * C, C), :].rearrange("p c d -> p (c d)"), fs[:, 10:11], C * HID, f_q,
                       i * (4 + C) + 4)
                dve.wait_ge(f_q, i + 1)
                for c in range(C):
                    xc = xa[:, bass.ds(i * C + c, 1), :].rearrange("p o d -> p (o d)")
                    TT(xc, xc, fb[:], ALU.add).then_inc(f_xb, 1)
                dve.wait_ge(f_mm, i + 1)
                dve.wait_ge(f_xb, i * (4 + C) + 8 + C)
                for c in range(C):
                    xc = xa[:, bass.ds(i * C + c, 1), :].rearrange("p o d -> p (o d)")
                    STT(out=xc, in0=X[c // 2][:, (c % 2) * HID:(c % 2 + 1) * HID], scalar=fs[:, 12:13], in1=xc,
                        op0=ALU.mult, op1=ALU.add).then_inc(f_out, 1)

        @block.gpsimd
        def _(pool):
            gp = nc.gpsimd
            pool.wait_ge(ones_set, 3)
            with pool.Fori(0, BLOCKS) as i:
                pool.wait_ge(pr_var, i + 1)
                gp.tensor_tensor(rstd[:], var[:], half[:], ALU.pow).then_inc(pr_rstd, 1)
            pool.wait_ge(pr_bset, 1)
            for s_ in (proj, packs, wss, cpow, cperm, mcs, lsum, utr, kvtr, stps, sktr, qk, sc, strn, atrn, pps,
                       ops, gps, rss, rpow, wops):
                pool.sem_inc(s_.handle, 2 * s_.per)

            def pack(g, blk, t, i, side):
                hold(pool, "pool", silu.handle, silu.at(g, blk, i + 1))
                for q, s in enumerate(LEVELS):
                    gp.tensor_copy(packed(pk[:, t], 64 * q, s), side(y[:, i, :], s)).then_inc(packs.handle, 1)

            def front_a(g, blk):
                pack(g, blk, 1, 0, right)
                pack(g, blk, 0, 1, left)
                pack(g, blk, 2, 2, left)

            def w_power(g, blk):
                pool.wait_ge(cv.handle, cv.at(g, blk, 1))
                gp.tensor_tensor(cpw[:], cvv[:], half[:], ALU.pow).then_inc(cpow.handle, 1)

            def masks(g, blk):
                pool.wait_ge(call.handle, call.at(g, blk, 2))
                pool.wait_ge(pevc.handle, pevc.at(g, blk - 1, 4))
                gp.tensor_tensor(
                    mc[:].rearrange("p c (q m) -> p c q m", q=3),
                    mask[:].rearrange("p (q m) -> p q m", q=3).unsqueeze(1).broadcast_to([P, C, 3, P]),
                    cc[:].rearrange("p q c -> p c q").unsqueeze(3).broadcast_to([P, C, 3, P]),
                    ALU.mult).then_inc(mcs.handle, 1)

            def r_power(g, blk):
                pool.wait_ge(rsv.handle, rsv.at(g, blk, 2))
                gp.tensor_tensor(rr[:], r1[:], half[:], ALU.pow).then_inc(rpow.handle, 1)

            def out_weights(g):
                hold(pool, "pool", w2_in, g * 48 + 48)
                gp.tensor_scalar(bgh[:], bg[:], 0.5, None, ALU.mult)
                gp.tensor_scalar(wos[:], wo[:], nwh[:, 0:1], None, ALU.mult).then_inc(wos_set, 1)

            def first():
                front_a(0, 0)
                w_power(0, 0)
                masks(0, 0)

            def slot(g, blk, more):
                if blk == 0:
                    out_weights(g)
                if more:
                    front_a(g, blk + 1)
                r_power(g, blk)
                if more:
                    w_power(g, blk + 1)
                    masks(g, blk + 1)

            run(pool, slot, first)

            with pool.Fori(0, BLOCKS) as i:
                pool.wait_ge(f_var, i + 1)
                gp.tensor_tensor(frstd[:], fvar[:], half[:], ALU.pow).then_inc(f_rstd, 1)
            pool.wait_ge(f_amax, 2)
            gp.partition_all_reduce(fs[:, 6:8], fs[:, 4:6], P, RMAX).then_inc(f_all, 1)


def constants():
    import numpy as np

    i = np.arange(P)[:, None]
    t = np.arange(P)[None, :]

    def lefts(s):
        return np.array([j for j in range(P) if (j // s) % 2 == 0])

    def rights(s):
        return np.array([j for j in range(P) if (j // s) % 2 == 1])

    incl = (i <= t)
    ref = t // DIAG * DIAG + REF
    diag = ((i > ref) & (i <= t)).astype(np.float32) - ((i > t) & (i <= ref)).astype(np.float32)
    right = []
    left = []
    for s in LEVELS:
        r = rights(s)[None, :]
        right.append((i >= r // s * s) & (i <= r))
        q = lefts(s)[None, :]
        left.append((i > q) & (i < (q // s + 1) * s))
    suf = i > t
    msum = np.concatenate([incl, diag, *right, suf, *left], 1).astype(np.float32)

    mask = np.zeros((P, 384), np.float32)
    perm = np.zeros((P, 2, P), np.float32)
    for v, s in enumerate(LEVELS):
        q, h = v // 2, v % 2
        jl, tr_ = lefts(s), rights(s)
        same = (jl[:, None] // (2 * s)) == (tr_[None, :] // (2 * s))
        mask[h * 64:(h + 1) * 64, q * P + h * 64:q * P + (h + 1) * 64] = same
        perm[jl, q, h * 64 + np.arange(64)] = 1.0
    mask[:, 256:384] = (i <= t) & (i // DIAG == t // DIAG)
    return msum, mask, perm, np.eye(P, dtype=np.float32)


def kernel(**inputs):
    import numpy as np
    import concourse.bacc as bacc
    from concourse.bass_utils import run_bass_kernel_spmd

    def get(name):
        return np.ascontiguousarray(inputs["L0_" + name])

    def heads(w):
        return w.reshape(KT, P, H, P).transpose(2, 1, 0, 3)

    def taps(w):
        return w.reshape(H, P, TAPS)

    msum, mask, perm, eye = constants()
    wqkvw = np.stack([heads(get("attn_W" + n)) for n in "qkvw"], 3).reshape(H, P, KT * 4 * P)
    conv = np.stack([taps(get("attn_c" + n)) for n in "qkvv"], 2).reshape(H, P, 4 * TAPS)
    rows = lambda w: w.reshape(KT, P, -1).transpose(1, 0, 2)
    arrays = {
        "x": get("attn_hidden_states").reshape(TOK, HID),
        "wqkvw": wqkvw,
        "conv": conv,
        "wf1": rows(get("attn_Wf1")),
        "wf2": get("attn_Wf2"),
        "wb": rows(get("attn_Wb")),
        "wg1": rows(get("attn_Wg1")),
        "wg2": get("attn_Wg2").reshape(P, H, P).transpose(1, 0, 2),
        "bg": get("attn_bg2").reshape(H, P, 1),
        "nw": get("attn_norm_w").reshape(P, 1),
        "wo": get("attn_Wo").reshape(H, P, HID),
        "fw": get("ffn_weight"),
        "fb": get("ffn_bias"),
        "msum": msum,
        "mask": mask,
        "perm": perm,
        "eye": eye,
    }
    arrays = {k: np.ascontiguousarray(v) for k, v in arrays.items()}
    nc = bacc.Bacc("TRN2", target_bir_lowering=False, num_devices=1)
    args = [nc.dram_tensor("in_" + k, v.shape, mybir.dt.from_np(v.dtype), kind="ExternalInput").ap()
            for k, v in arrays.items()]
    out = nc.dram_tensor("out_0", (TOK, HID), F32, kind="ExternalOutput").ap()
    hT_d = nc.dram_tensor("hT_d", (BLOCKS, P, KT * NT), F32, kind="Internal").ap()
    h1_d = nc.dram_tensor("h1_d", (BLOCKS, P, NT), F32, kind="Internal").ap()
    g_d = nc.dram_tensor("g_d", (H, BLOCKS, P, NT), F32, kind="Internal").ap()
    program(nc, *args, out, hT_d, h1_d, g_d)
    r = run_bass_kernel_spmd(nc, [{"in_" + k: v for k, v in arrays.items()}], core_ids=[0])
    return r.results[0]["out_0"].reshape(TOK // SEQ, SEQ, HID)
```

```python
from contextlib import ExitStack

import concourse.bass as bass
from concourse import mybir

ALU = mybir.AluOpType
ACT = mybir.ActivationFunctionType
F32 = mybir.dt.float32
BF16 = mybir.dt.bfloat16
F32R = mybir.dt.float32r
U32 = mybir.dt.uint32
AX = mybir.AxisListType
RMAX = bass.bass_isa.ReduceOp.max

P = 128
HID = 256
KT = HID // P
H = 16
TOK = 4096
SEQ = 2048
C = 4
NT = C * P
BLOCKS = TOK // NT
UN = SEQ // NT
GROUPS = H * TOK // SEQ
CHUNKS = TOK // P
TAPS = 4
ORDER = (3, 1, 0, 2)
LEVELS = (64, 32, 16, 8)
DIAG = 8
REF = DIAG // 2 - 1
ZMIN = -20.0
SCALE = float(P) ** -0.5
SC = SCALE / 4.0
EPS = 1e-5
L2EPS = 1e-6
QMAX = 448.0 * 0.8

NR = 4 * 64
INCL, DPOS, RIGHT = 0, P, 2 * P
SUF, LEFT, DNEG = 0, P, P + NR


class Steps:

    def __init__(self, handle, per):
        self.handle, self.per = handle, per

    def at(self, g, blk, k):
        return g * (UN * self.per) + (blk + 2) * self.per + k


def program(nc, x_d, wqkvw_d, conv_d, wf1_d, wf2_d, wb_d, wg1_d, wg2_d, bg_d, nw_d, wo_d, fw_d, fb_d,
            msum_d, mask_d, perm_d, eye_d, out_d, hT_d, h1_d, g_d):
    ctx = ExitStack()
    with ctx:
        def sb(name, shape, dt=F32, stack=ctx):
            return stack.enter_context(nc.sbuf_tensor(name, shape, dt))

        def sem(name):
            return ctx.enter_context(nc.semaphore(name))

        def steps(name, per):
            return Steps(sem(name), per)

        bank = [ctx.enter_context(nc.psum_tensor(f"bank{i}", [P, 512], F32)) for i in range(8)]
        X, L, Z, S, O = bank[0:2], bank[2:4], bank[4:6], bank[6], bank[7]

        xa = sb("xa", [P, CHUNKS, HID])
        msr = sb("msr", [P, 896], F32R)
        mask = sb("mask", [P, 384])
        perm = sb("perm", [P, 2, P])
        eye = sb("eye", [P, P])
        eyeb = sb("eyeb", [P, P], BF16)
        ones = sb("ones", [P, 1])
        half = sb("half", [P, 4])
        beta = sb("beta", [P, H, CHUNKS])
        nwh = sb("nwh", [P, 1])
        nw = sb("nw", [P, 1])

        const_in = sem("const_in")
        x_in = sem("x_in")
        ones_set = sem("ones_set")
        pr_stat = sem("pr_stat")
        pr_aggr = sem("pr_aggr")
        pr_var = sem("pr_var")
        pr_rstd = sem("pr_rstd")
        pr_h = sem("pr_h")
        pr_tr = sem("pr_tr")
        pr_hT = sem("pr_hT")
        pr_low = sem("pr_low")
        pr_lowc = sem("pr_lowc")
        pr_beta = sem("pr_beta")
        pr_betac = sem("pr_betac")
        pr_z = sem("pr_z")
        pr_zc = sem("pr_zc")
        pr_exp = sem("pr_exp")
        pr_ln = sem("pr_ln")
        pr_st = sem("pr_st")
        pr_sg = sem("pr_sg")
        pr_tanh = sem("pr_tanh")
        pr_bset = sem("pr_bset")

        ht_in = [sem(f"ht_in{i}") for i in range(2)]
        g_in = [sem(f"g_in{i}") for i in range(2)]
        h1_in = [sem(f"h1_in{i}") for i in range(2)]
        w_in = sem("w_in")
        w2_in = sem("w2_in")
        proj = steps("proj", 4)
        halo = steps("halo", 4)
        pevac = steps("pevac", 8)
        conv = steps("conv", 12)
        tanh = steps("tanh", 4)
        silu = steps("silu", 4)
        kpacks = steps("kpacks", 4)
        qpacks = steps("qpacks", 4)
        vpacks = steps("vpacks", 4)
        wsq = steps("wsq", 1)
        wss = steps("wss", 1)
        cv = steps("cv", 1)
        cpow = steps("cpow", 1)
        cnat = steps("cnat", 1)
        cperm = steps("cperm", 1)
        call = steps("call", 1)
        mcs = steps("mcs", 1)
        gpart = steps("gpart", 2)
        lsum = steps("lsum", 8)
        expA = steps("expA", 8)
        expB = steps("expB", 4)
        wprod = steps("wprod", 6)
        utr = steps("utr", 4)
        uevac = steps("uevac", 8)
        kvtr = steps("kvtr", 4)
        kvevac = steps("kvevac", 4)
        stps = steps("stps", 4)
        st0 = steps("st0", 1)
        stupd = steps("stupd", 4)
        sktr = steps("sktr", 1)
        skevac = steps("skevac", 1)
        qk = steps("qk", 4)
        aevac = steps("aevac", 4)
        sc = steps("sc", 4)
        prods = steps("prods", 4)
        adds = steps("adds", 5)
        strn = steps("strn", 1)
        smax = steps("smax", 1)
        nmax = steps("nmax", 1)
        sexp = steps("sexp", 4)
        atrn = steps("atrn", 1)
        aes = steps("aes", 5)
        pps = steps("pps", 4)
        pevc = steps("pevc", 4)
        ops = steps("ops", 1)
        gps = steps("gps", 1)
        gth = steps("gth", 1)
        osqs = steps("osqs", 1)
        ogs = steps("ogs", 1)
        rss = steps("rss", 1)
        rsv = steps("rsv", 2)
        rpow = steps("rpow", 1)
        wops = steps("wops", 2)
        oacc = steps("oacc", 4)
        wos_set = sem("wos_set")

        f_in = sem("f_in")
        f_stat = sem("f_stat")
        f_aggr = sem("f_aggr")
        f_var = sem("f_var")
        f_rstd = sem("f_rstd")
        f_y = sem("f_y")
        f_mx = sem("f_mx")
        f_wmx = sem("f_wmx")
        f_amax = sem("f_amax")
        f_all = sem("f_all")
        f_sc = sem("f_sc")
        f_q = sem("f_q")
        f_wq = sem("f_wq")
        f_tr = sem("f_tr")
        f_trc = sem("f_trc")
        f_mm = sem("f_mm")
        f_out = sem("f_out")
        f_xb = sem("f_xb")
        f_st = sem("f_st")

        pro = ExitStack()
        msum = sb("msum", [P, 896], stack=pro)
        wf1 = sb("wf1", [P, KT, P], stack=pro)
        wg1 = sb("wg1", [P, KT, P], stack=pro)
        wf2 = sb("wf2", [P, H * P], stack=pro)
        wb = sb("wb", [P, KT, H], stack=pro)
        stat = sb("stat", [P, C, 6], stack=pro)
        mv = sb("mv", [P, C, 2], stack=pro)
        var = sb("var", [P, C], stack=pro)
        rstd = sb("rstd", [P, C], stack=pro)
        hn = sb("hn", [P, C, HID], stack=pro)
        hTb = sb("hTb", [P, KT, NT], stack=pro)
        low = sb("low", [P, 2, NT], stack=pro)
        zs = sb("zs", [P, C, H * P], stack=pro)
        braw = sb("braw", [P, H, CHUNKS], stack=pro)
        pro.close()

        mn = ExitStack()
        hT = sb("hT", [P, 2, KT, NT], stack=mn)
        h1 = sb("h1", [P, 2, NT], stack=mn)
        gl = sb("gl", [P, 2, NT], stack=mn)
        gh = sb("gh", [P, NT], F32R, stack=mn)
        gr = sb("gr", [P, NT], F32R, stack=mn)
        wh = sb("wh", [P, KT, 4, P], stack=mn)
        cw = sb("cw", [P, 4, TAPS], stack=mn)
        wg2 = sb("wg2", [P, P], stack=mn)
        wo = sb("wo", [P, HID], stack=mn)
        wos = sb("wos", [P, HID], stack=mn)
        bg = sb("bg", [P, 1], stack=mn)
        bgh = sb("bgh", [P, 1], stack=mn)
        xb = sb("xb", [P, 4, NT + 4], stack=mn)
        y = sb("y", [P, 4, NT], stack=mn)
        th = sb("th", [P, 2, NT], stack=mn)
        pk = sb("pk", [P, 3, C, NR], stack=mn)
        ysq = sb("ysq", [P, NT], stack=mn)
        cvv = sb("cvv", [P, C], stack=mn)
        cpw = sb("cpw", [P, C], stack=mn)
        cc = sb("cc", [P, 3, C], stack=mn)
        mc = sb("mc", [P, C, 384], stack=mn)
        ERs = [sb(f"ER{i}", [P, C, 512], stack=mn) for i in range(2)]
        ELs = [sb(f"EL{i}", [P, C, 512], stack=mn) for i in range(2)]
        U = sb("U", [P, C, 512], stack=mn)
        kv = sb("kv", [P, C, 512], stack=mn)
        ST = sb("ST", [P, C + 1, 2 * P], stack=mn)
        Sk = sb("Sk", [P, C, P], stack=mn)
        A = sb("A", [P, C, 384], stack=mn)
        pr = sb("pr", [P, C, 512], stack=mn)
        mx = sb("mx", [P, C], stack=mn)
        nm = sb("nm", [P, C], stack=mn)
        den = sb("den", [P, C], stack=mn)
        a = sb("a", [P, C, P], stack=mn)
        Pm = A
        gt = sb("gt", [P, NT], stack=mn)
        AE = pr
        osq = sb("osq", [P, NT], stack=mn)
        og = sb("og", [P, NT], stack=mn)
        r0 = sb("r0", [P, C], stack=mn)
        r1 = sb("r1", [P, C], stack=mn)
        rr = sb("rr", [P, C], stack=mn)
        mn.close()

        ff = ExitStack()
        fy = sb("fy", [P, CHUNKS, HID], stack=ff)
        fq = sb("fq", [P, CHUNKS, HID], BF16, stack=ff)
        fu = sb("fu", [P, C * HID], stack=ff)
        fm = sb("fm", [P, C * HID], stack=ff)
        fstat = sb("fstat", [P, C, 6], stack=ff)
        fmv = sb("fmv", [P, C, 2], stack=ff)
        fvar = sb("fvar", [P, C], stack=ff)
        frstd = sb("frstd", [P, C], stack=ff)
        fhi = sb("fhi", [P, BLOCKS], stack=ff)
        flo = sb("flo", [P, BLOCKS], stack=ff)
        fw = sb("fw", [P, KT, HID], stack=ff)
        fwq = sb("fwq", [P, KT, HID], BF16, stack=ff)
        fwT = sb("fwT", [P, KT, HID], BF16, stack=ff)
        fb = sb("fb", [P, HID], stack=ff)
        fs = sb("fs", [P, 16], stack=ff)
        fqT = sb("fqT", [P, C, KT, P], BF16, stack=ff)
        fo = sb("fo", [P, 2, C, HID], stack=ff)
        ff.close()

        passed = {name: sem("passed_" + name) for name in ("sp", "dve", "pool")}

        def hold(eng, name, handle, value):
            eng.wait_ge(handle, value)
            eng.sem_inc(passed[name], 1)

        block = ctx.enter_context(nc.Block())

        def left(t, s):
            return t.rearrange("p (c n two s) -> p c n two s", c=C, two=2, s=s)[:, :, :, 0, :]

        def right(t, s):
            return t.rearrange("p (c n two s) -> p c n two s", c=C, two=2, s=s)[:, :, :, 1, :]

        def packed(t, col, s):
            return t[:, :, col:col + 64].rearrange("p c (n s) -> p c n s", s=s)

        def par(blk):
            return blk % 2

        def loads(g, blk):
            return g * (16 * UN // 2) + 16 * (blk // 2 + 1)

        def run(eng, slot, first):
            first()
            with eng.Fori(0, GROUPS - 1) as g:
                for blk in range(UN):
                    slot(g, blk, True)
            for blk in range(UN):
                slot(GROUPS - 1, blk, blk < UN - 1)

        @block.sync
        def _(sp):
            for dst, src in ((msum, msum_d), (mask, mask_d), (perm, perm_d), (eye, eye_d), (nw, nw_d),
                             (wf1, wf1_d), (wg1, wg1_d), (wf2, wf2_d), (wb, wb_d)):
                sp.dma_start(dst[:], src).then_inc(const_in, 16)
            with sp.Fori(0, BLOCKS) as i:
                sp.dma_start(xa[:, bass.ds(i * C, C), :],
                             x_d[bass.ds(i * NT, NT), :].rearrange("(c p) d -> p c d", p=P)).then_inc(x_in, 16)
                hold(sp, "sp", x_in, i * 16 + 16)
            with sp.Fori(0, BLOCKS) as i:
                hold(sp, "sp", pr_hT, i * 2 + 2)
                sp.dma_start(hT_d[bass.ds(i, 1)].rearrange("o p n -> (o p) n"),
                             hTb[:].rearrange("p k n -> p (k n)")).then_inc(pr_st, 16)
                hold(sp, "sp", pr_lowc, i * 2 + 2)
                sp.dma_start(h1_d[bass.ds(i, 1)].rearrange("o p n -> (o p) n"), low[:, 1, :]).then_inc(pr_st, 16)
                hold(sp, "sp", pr_ln, i * 16 + 16)
                for b in range(2):
                    for c in range(C):
                        sp.dma_start(
                            g_d[b * 8:b * 8 + 8, bass.ds(i, 1), :, c * P:(c + 1) * P].rearrange(
                                "h o p m -> (o p) h m"),
                            zs[:, c, b * 8 * P:(b + 1) * 8 * P].rearrange("p (h m) -> p h m", m=P)
                        ).then_inc(pr_sg, 16)
            hold(sp, "sp", pr_st, BLOCKS * 32)
            hold(sp, "sp", pr_sg, BLOCKS * 128)
            hold(sp, "sp", pr_bset, 1)

            def load_block(g, blk, static):
                p = par(blk)
                n8 = (g % 2) * UN + blk if static else (g % 2) * UN + blk
                hold(sp, "sp", proj.handle, proj.at(g, blk - 2, 4))
                sp.dma_start(hT[:, p].rearrange("p k n -> p (k n)"),
                             hT_d[bass.ds(n8, 1)].rearrange("o p n -> (o p) n")).then_inc(ht_in[p], 16)
                hold(sp, "sp", gpart.handle, gpart.at(g, blk - 2, 2))
                hh = g // 2
                sp.dma_start(gl[:, p, :],
                             g_d[bass.ds(hh, 1), bass.ds(n8, 1)].rearrange("a o p m -> (a o p) m")
                             ).then_inc(g_in[p], 16)
                if blk == 0:
                    hold(sp, "sp", proj.handle, proj.at(g, -1, 4))
                    hold(sp, "sp", conv.handle, conv.at(g, -1, 12))
                    sp.dma_start(wh[:].rearrange("p k a n -> p (k a n)"),
                                 wqkvw_d[bass.ds(hh, 1)].rearrange("o p n -> (o p) n")).then_inc(w_in, 16)
                    sp.dma_start(cw[:].rearrange("p a t -> p (a t)"),
                                 conv_d[bass.ds(hh, 1)].rearrange("o p n -> (o p) n")).then_inc(w_in, 16)
                    hold(sp, "sp", wops.handle, wops.at(g, -1, 2))
                    hold(sp, "sp", gth.handle, gth.at(g, -1, 1))
                    for dst, src in ((wg2, wg2_d), (wo, wo_d), (bg, bg_d)):
                        sp.dma_start(dst[:], src[bass.ds(hh, 1)].rearrange("o p n -> (o p) n")
                                     ).then_inc(w2_in, 16)
                hold(sp, "sp", gps.handle, gps.at(g, blk - 2, 1))
                sp.dma_start(h1[:, p, :], h1_d[bass.ds(n8, 1)].rearrange("o p n -> (o p) n")
                             ).then_inc(h1_in[p], 16)

            with sp.Fori(0, GROUPS) as g:
                for blk in range(UN):
                    load_block(g, blk, False)

            hold(sp, "sp", oacc.handle, oacc.at(GROUPS - 1, UN - 1, 4))
            sp.dma_start(fw[:], fw_d.rearrange("(a p) d -> p a d", p=P)).then_inc(f_in, 16)
            sp.dma_start(fb[:], fb_d.rearrange("(a d) -> a d", a=1).broadcast_to([P, HID])).then_inc(f_in, 16)
            with sp.Fori(0, BLOCKS) as i:
                hold(sp, "sp", f_out, i * C + C)
                sp.dma_start(out_d[bass.ds(i * NT, NT), :].rearrange("(c p) d -> p c d", p=P),
                             xa[:, bass.ds(i * C, C), :]).then_inc(f_st, 16)
            hold(sp, "sp", f_st, BLOCKS * 16)

        @block.tensor
        def _(pe):
            mm = nc.tensor.matmul
            tr = nc.tensor.transpose

            pe.wait_ge(const_in, 16 * 9)
            with pe.Fori(0, BLOCKS) as i:
                pe.wait_ge(pr_h, i * C + C)
                pe.wait_ge(pr_hT, i * 2)
                for k in range(KT):
                    for c in range(C):
                        t = tr(Z[k][:, c * P:(c + 1) * P], hn[:, c, k * P:(k + 1) * P], eye[:])
                    t.then_inc(pr_tr, 1)
                pe.wait_ge(pr_hT, i * 2 + 2)
                for j, w in enumerate((wf1, wg1)):
                    if j == 0:
                        pe.wait_ge(pr_lowc, i * 2)
                    for k in range(KT):
                        t = mm(X[j][:], lhsT=w[:, k, :], rhs=hTb[:, k, :], start=k == 0, stop=k == KT - 1)
                    t.then_inc(pr_low, 1)
                pe.wait_ge(pr_betac, i)
                for c in range(C):
                    for k in range(KT):
                        t = mm(O[:, c * H:(c + 1) * H], lhsT=hTb[:, k, c * P:(c + 1) * P], rhs=wb[:, k, :],
                               start=k == 0, stop=k == KT - 1)
                t.then_inc(pr_beta, 1)
                pe.wait_ge(pr_lowc, i * 2 + 1)
                for c in range(C):
                    for j in range(4):
                        q = c * 4 + j
                        if q < 2:
                            pe.wait_ge(pr_zc, i * 16)
                        else:
                            pe.wait_ge(pr_zc, i * 16 + q - 1)
                        mm(L[q % 2][:], lhsT=low[:, 0, c * P:(c + 1) * P], rhs=wf2[:, j * 512:(j + 1) * 512],
                           start=True, stop=True).then_inc(pr_z, 1)
            pe.wait_ge(pr_bset, 1)

            def project(g, blk, i):
                if i == 0:
                    if blk % UN == 0:
                        pe.wait_ge(w_in, g * 32 + (blk // UN) * 32 + 32)
                    pe.wait_ge(ht_in[par(blk)], loads(g, blk))
                    pe.wait_ge(aevac.handle, aevac.at(g, blk - 1, 3))
                elif i == 1:
                    pe.wait_ge(gth.handle, gth.at(g, blk - 1, 1))
                else:
                    pe.wait_ge(pevac.handle, pevac.at(g, blk, 2 * (i - 2) + 2))
                for k in range(KT):
                    t = mm(X[(i + 1) % 2][:], lhsT=wh[:, k, ORDER[i], :], rhs=hT[:, par(blk), k, :],
                           start=k == 0, stop=k == KT - 1)
                t.then_inc(proj.handle, 1)

            def step_sums(g, blk, c):
                if c == 0:
                    pe.wait_ge(gpart.handle, gpart.at(g, blk, 2))
                    pe.wait_ge(prods.handle, prods.at(g, blk - 1, 4))
                else:
                    pe.wait_ge(expA.handle, expA.at(g, blk, 2 * c))
                for w, part in ((gh, 0), (gr, 1)):
                    t = mm(L[0][:], lhsT=w[:, c * P:(c + 1) * P], rhs=msr[:, 0:512], start=part == 0, stop=part == 1)
                t.then_inc(lsum.handle, 1)
                if c > 0:
                    pe.wait_ge(expB.handle, expB.at(g, blk, c))
                for w, part in ((gh, 0), (gr, 1)):
                    t = mm(L[1][:, 0:384], lhsT=w[:, c * P:(c + 1) * P], rhs=msr[:, 512:896],
                           start=part == 0, stop=part == 1)
                t.then_inc(lsum.handle, 1)

            def w_norms(g, blk):
                pe.wait_ge(wsq.handle, wsq.at(g, blk, 1))
                for c in range(C):
                    t = mm(S[:, 256 + c:257 + c], lhsT=ysq[:, c * P:(c + 1) * P], rhs=ones[:], start=True, stop=True)
                t.then_inc(wss.handle, 1)

            def w_permuted(g, blk):
                pe.wait_ge(rsv.handle, rsv.at(g, blk - 1, 2))
                pe.wait_ge(cnat.handle, cnat.at(g, blk, 1))
                for q in range(2):
                    t = mm(S[:, 260 + q * C:260 + (q + 1) * C], lhsT=perm[:, q, :], rhs=cc[:, 2, :],
                           start=True, stop=True)
                t.then_inc(cperm.handle, 1)

            def qk_products(g, blk, c):
                if c == 0:
                    pe.wait_ge(kpacks.handle, kpacks.at(g, blk, 4))
                    pe.wait_ge(qpacks.handle, qpacks.at(g, blk, 4))
                if c < 2:
                    pe.wait_ge(pevac.handle, pevac.at(g, blk, 2 * (c + 2) + 2))
                else:
                    pe.wait_ge(aevac.handle, aevac.at(g, blk, c - 1))
                b = X[(c + 1) % 2]
                for q in range(2):
                    mm(b[:, q * P:(q + 1) * P], lhsT=pk[:, 0, c, q * P:(q + 1) * P],
                       rhs=pk[:, 1, c, q * P:(q + 1) * P], start=True, stop=True)
                mm(b[:, 256:384], lhsT=y[:, 1, c * P:(c + 1) * P], rhs=y[:, 0, c * P:(c + 1) * P],
                   start=True, stop=True).then_inc(qk.handle, 1)

            def kv_transposes(g, blk, c):
                if c == 0:
                    pe.wait_ge(vpacks.handle, vpacks.at(g, blk, 4))
                if c < 2:
                    pe.wait_ge(oacc.handle, oacc.at(g, blk - 1, 2 * c + 2))
                else:
                    pe.wait_ge(kvevac.handle, kvevac.at(g, blk, c - 1))
                tr(Z[c % 2][:, 0:P], y[:, 1, c * P:(c + 1) * P], eye[:])
                tr(Z[c % 2][:, P:2 * P], y[:, 2, c * P:(c + 1) * P], eye[:])
                tr(Z[c % 2][:, 2 * P:3 * P], pk[:, 2, c, 0:P], eye[:])
                tr(Z[c % 2][:, 3 * P:4 * P], pk[:, 2, c, P:2 * P], eye[:]).then_inc(kvtr.handle, 1)

            def u_transposes(g, blk, c):
                el = ELs[par(blk)]
                if c == 0:
                    pe.wait_ge(wprod.handle, wprod.at(g, blk, 6))
                if c < 2:
                    pe.wait_ge(kvevac.handle, kvevac.at(g, blk, c + 3))
                else:
                    pe.wait_ge(uevac.handle, uevac.at(g, blk, 2 * (c - 1)))
                for q in range(4):
                    t = tr(Z[c % 2][:, q * P:(q + 1) * P], el[:, c, q * P:(q + 1) * P], eye[:])
                t.then_inc(utr.handle, 1)

            def states(g, blk, c):
                if c == 0:
                    pe.wait_ge(call.handle, call.at(g, blk, 1))
                pe.wait_ge(uevac.handle, uevac.at(g, blk, 2 * c + 2))
                if c > 0:
                    pe.wait_ge(stupd.handle, stupd.at(g, blk, c))
                mm(S[:, 0:256], lhsT=U[:, c, 0:P], rhs=kv[:, c, 0:256], start=True, stop=True
                   ).then_inc(stps.handle, 1)

            def state_transposes(g, blk):
                pe.wait_ge(stupd.handle, stupd.at(g, blk, 3))
                for c in range(C):
                    t = tr(Z[0][:, c * P:(c + 1) * P], ST[:, c, 0:P], eye[:])
                t.then_inc(sktr.handle, 1)

            def scores_in_chunk(g, blk, c):
                pe.wait_ge(aevac.handle, aevac.at(g, blk, c + 1))
                if c == 0:
                    pe.wait_ge(expA.handle, expA.at(g, blk, 8))
                elif c == 1:
                    pe.wait_ge(expB.handle, expB.at(g, blk, 4))
                else:
                    pe.wait_ge(prods.handle, prods.at(g, blk, c - 1))
                mm(L[c % 2][:, P:2 * P], lhsT=U[:, c, DNEG:DNEG + P], rhs=A[:, c, 256:384],
                   start=True, stop=True)
                for q in range(2):
                    mm(L[c % 2][:, (2 + q) * P:(3 + q) * P], lhsT=U[:, c, (1 + q) * P:(2 + q) * P],
                       rhs=A[:, c, q * P:(q + 1) * P], start=True, stop=True)

            def scores_from_state(g, blk, c):
                if c == 0:
                    pe.wait_ge(skevac.handle, skevac.at(g, blk, 1))
                mm(L[c % 2][:, 0:P], lhsT=Sk[:, c, :], rhs=y[:, 0, c * P:(c + 1) * P], start=True, stop=True
                   ).then_inc(sc.handle, 1)

            def score_transposes(g, blk):
                pe.wait_ge(adds.handle, adds.at(g, blk, 5))
                for c in range(C):
                    t = tr(Z[0][:, c * P:(c + 1) * P], pr[:, c, 0:P], eye[:])
                t.then_inc(strn.handle, 1)

            def gate_product(g, blk):
                if blk == 0:
                    pe.wait_ge(w2_in, g * 48 + 48)
                pe.wait_ge(h1_in[par(blk)], loads(g, blk))
                pe.wait_ge(aevac.handle, aevac.at(g, blk, 4))
                mm(X[0][:], lhsT=wg2[:], rhs=h1[:, par(blk), :], start=True, stop=True).then_inc(gps.handle, 1)

            def a_transposes(g, blk):
                pe.wait_ge(sexp.handle, sexp.at(g, blk, 4))
                for c in range(C):
                    t = tr(Z[1][:, c * P:(c + 1) * P], a[:, c, :], eye[:])
                t.then_inc(atrn.handle, 1)

            def p_products(g, blk):
                pe.wait_ge(aes.handle, aes.at(g, blk, 5))
                for c in range(C):
                    if c >= 2:
                        pe.wait_ge(pevc.handle, pevc.at(g, blk, c - 1))
                    b = Z[c % 2]
                    el = ELs[par(blk)]
                    for q in range(2):
                        mm(b[:, q * P:(q + 1) * P], lhsT=el[:, c, (1 + q) * P:(2 + q) * P],
                           rhs=AE[:, c, (2 + q) * P:(3 + q) * P], start=True, stop=True)
                    mm(b[:, 256:384], lhsT=el[:, c, DNEG:DNEG + P], rhs=AE[:, c, DPOS:DPOS + P],
                       start=True, stop=True).then_inc(pps.handle, 1)

            def o_products(g, blk):
                for c in range(C):
                    oc = O[:, c * P:(c + 1) * P]
                    mm(oc, lhsT=ST[:, c, P:2 * P], rhs=AE[:, c, INCL:INCL + P], start=True, stop=False)
                    pe.wait_ge(pevc.handle, pevc.at(g, blk, c + 1))
                    mm(oc, lhsT=kv[:, c, P:2 * P], rhs=Pm[:, c, 256:384], start=False, stop=False)
                    for v, s in enumerate(LEVELS):
                        orr = oc.rearrange("p (n two s) -> p n two s", two=2, s=s)[:, :, 1, :]
                        t = mm(orr, lhsT=kv[:, c, (2 + v // 2) * P:(3 + v // 2) * P],
                               rhs=Pm[:, c, v * 64:(v + 1) * 64].rearrange("p (n s) -> p n s", s=s),
                               start=False, stop=v == 3)
                t.then_inc(ops.handle, 1)

            def o_norms(g, blk, more):
                pe.wait_ge(osqs.handle, osqs.at(g, blk, 1))
                if more:
                    pe.wait_ge(cv.handle, cv.at(g, blk + 1, 1))
                for c in range(C):
                    t = mm(S[:, 268 + c:269 + c], lhsT=osq[:, c * P:(c + 1) * P], rhs=ones[:], start=True, stop=True)
                t.then_inc(rss.handle, 1)

            def out_products(g, blk):
                pe.wait_ge(ogs.handle, ogs.at(g, blk, 1))
                if blk == 0:
                    pe.wait_ge(wos_set, g + 1)
                for j in range(2):
                    pe.wait_ge(pevc.handle, pevc.at(g, blk, 3 + j))
                    for c in range(2):
                        t = mm(Z[j][:, c * HID:(c + 1) * HID],
                               lhsT=og[:, (2 * j + c) * P:(2 * j + c + 1) * P], rhs=wos[:], start=True, stop=True)
                    t.then_inc(wops.handle, 1)

            def front_b(g, blk):
                for c in range(C):
                    kv_transposes(g, blk, c)
                u_transposes(g, blk, 0)
                qk_products(g, blk, 2)
                u_transposes(g, blk, 1)
                qk_products(g, blk, 3)
                states(g, blk, 0)
                u_transposes(g, blk, 2)
                states(g, blk, 1)
                u_transposes(g, blk, 3)
                scores_in_chunk(g, blk, 0)
                states(g, blk, 2)
                scores_in_chunk(g, blk, 1)
                states(g, blk, 3)
                state_transposes(g, blk)
                for c in range(C):
                    if c >= 2:
                        scores_in_chunk(g, blk, c)
                    scores_from_state(g, blk, c)

            def first():
                for i in range(4):
                    project(0, 0, i)
                    step_sums(0, 0, i)
                    if i == 0:
                        w_norms(0, 0)
                w_permuted(0, 0)
                qk_products(0, 0, 0)
                qk_products(0, 0, 1)
                front_b(0, 0)

            def slot(g, blk, more):
                gate_product(g, blk)
                if more:
                    project(g, blk + 1, 0)
                score_transposes(g, blk)
                if more:
                    project(g, blk + 1, 1)
                    step_sums(g, blk + 1, 0)
                a_transposes(g, blk)
                if more:
                    project(g, blk + 1, 2)
                p_products(g, blk)
                o_products(g, blk)
                if more:
                    w_norms(g, blk + 1)
                    step_sums(g, blk + 1, 1)
                o_norms(g, blk, more)
                if more:
                    project(g, blk + 1, 3)
                out_products(g, blk)
                if more:
                    step_sums(g, blk + 1, 2)
                    w_permuted(g, blk + 1)
                    step_sums(g, blk + 1, 3)
                    qk_products(g, blk + 1, 0)
                    qk_products(g, blk + 1, 1)
                    front_b(g, blk + 1)

            run(pe, slot, first)

            pe.wait_ge(f_wq, 1)
            zb = [Z[0][:].bitcast(BF16), Z[1][:].bitcast(BF16)]
            for k in range(KT):
                for o in range(KT):
                    t = tr(zb[0][:, (k * 2 + o) * P:(k * 2 + o + 1) * P], fwq[:, o, k * P:(k + 1) * P], eyeb[:])
            t.then_inc(f_tr, 1)
            pe.wait_ge(f_trc, 1)
            with pe.Fori(0, BLOCKS) as i:
                pe.wait_ge(f_q, i + 1)
                for c in range(C):
                    pe.wait_ge(f_out, i * C)
                    for k in range(KT):
                        t = tr(zb[1][:, (c * 2 + k) * P:(c * 2 + k + 1) * P],
                               fq[:, bass.ds(i * C + c, 1), k * P:(k + 1) * P].rearrange("p o n -> p (o n)"),
                               eyeb[:])
                t.then_inc(f_tr, 1)
                pe.wait_ge(f_trc, i + 2)
                for c in range(C):
                    for k in range(KT):
                        t = mm(X[c // 2][:, (c % 2) * HID:(c % 2 + 1) * HID], lhsT=fqT[:, c, k, :],
                               rhs=fwT[:, k, :], start=k == 0, stop=k == KT - 1)
                t.then_inc(f_mm, 1)

        @block.scalar
        def _(act):
            fn = nc.scalar.activation
            with act.Fori(0, BLOCKS) as i:
                act.wait_ge(pr_sg, i * 128)
                for q in range(16):
                    c, j = q // 4, q % 4
                    act.wait_ge(pr_zc, i * 16 + q + 1)
                    zz = zs[:, c, j * 512:(j + 1) * 512]
                    fn(zz, zz, ACT.Exp, scale=-1.0).then_inc(pr_exp, 1)
                for q in range(16):
                    c, j = q // 4, q % 4
                    act.wait_ge(pr_exp, i * 16 + q + 1)
                    zz = zs[:, c, j * 512:(j + 1) * 512]
                    fn(zz, zz, ACT.Ln, bias=1.0).then_inc(pr_ln, 1)
            act.wait_ge(pr_betac, BLOCKS)
            fn(beta[:], braw[:], ACT.Tanh, scale=0.5).then_inc(pr_tanh, 1)
            act.wait_ge(pr_bset, 1)
            for s_ in (halo, pevac, qpacks, vpacks, tanh, wsq, expA, expB, uevac, kvevac, skevac, sexp, gth, osqs):
                act.sem_inc(s_.handle, 2 * s_.per)

            def evacuate(g, blk, i):
                w = ORDER[i]
                act.wait_ge(conv.handle, conv.at(g, blk - 1, 3 * i + 3))
                if blk % UN == 0:
                    fn(xb[:, w, 1:4], eye[:, 0:3], ACT.Copy, scale=0.0).then_inc(halo.handle, 1)
                else:
                    nc.scalar.copy(xb[:, w, 1:4], xb[:, w, NT + 1:NT + 4]).then_inc(halo.handle, 1)
                if i == 0:
                    act.wait_ge(sc.handle, sc.at(g, blk - 1, 4))
                act.wait_ge(proj.handle, proj.at(g, blk, i + 1))
                act.wait_ge(halo.handle, halo.at(g, blk, i + 1))
                fn(xb[:, w, 4:NT + 4], X[(i + 1) % 2][:], ACT.Copy).then_inc(pevac.handle, 1)
                fn(y[:, w, :], X[(i + 1) % 2][:], ACT.Copy, scale=cw[:, w, 3:4]).then_inc(pevac.handle, 1)

            def half_tanh(g, blk, i):
                act.wait_ge(conv.handle, conv.at(g, blk, 3 * i + 3))
                act.wait_ge(silu.handle, silu.at(g, blk - 1, i + 3))
                fn(th[:, i % 2, :], y[:, ORDER[i], :], ACT.Tanh, scale=0.5).then_inc(tanh.handle, 1)

            def w_square(g, blk):
                act.wait_ge(silu.handle, silu.at(g, blk, 1))
                fn(ysq[:], y[:, 3, :], ACT.Square).then_inc(wsq.handle, 1)

            def pack_q(g, blk):
                act.wait_ge(silu.handle, silu.at(g, blk, 3))
                for q, s in enumerate(LEVELS):
                    fn(packed(pk[:, 1], 64 * q, s), right(y[:, 0, :], s), ACT.Copy).then_inc(qpacks.handle, 1)

            def pack_v(g, blk):
                act.wait_ge(silu.handle, silu.at(g, blk, 4))
                for q, s in enumerate(LEVELS):
                    fn(packed(pk[:, 2], 64 * q, s), left(y[:, 2, :], s), ACT.Copy).then_inc(vpacks.handle, 1)

            def decays(g, blk, c):
                er, el = ERs[par(blk)], ELs[par(blk)]
                if c == 0:
                    act.wait_ge(aes.handle, aes.at(g, blk - 2, 5))
                    act.wait_ge(pps.handle, pps.at(g, blk - 2, 4))
                act.wait_ge(lsum.handle, lsum.at(g, blk, 2 * c + 1))
                fn(er[:, c, :], L[0][:], ACT.Exp, scale=-1.0).then_inc(expA.handle, 1)
                fn(el[:, c, DNEG:DNEG + P], L[0][:, DPOS:DPOS + P], ACT.Exp).then_inc(expA.handle, 1)
                act.wait_ge(lsum.handle, lsum.at(g, blk, 2 * c + 2))
                fn(el[:, c, 0:384], L[1][:, 0:384], ACT.Exp, scale=-1.0).then_inc(expB.handle, 1)

            def u_copies(g, blk):
                act.wait_ge(call.handle, call.at(g, blk, 1))
                for c in range(C):
                    act.wait_ge(utr.handle, utr.at(g, blk, c + 1))
                    fn(U[:, c, 0:P], Z[c % 2][:, 0:P], ACT.Copy, scale=cc[:, 2, c:c + 1]).then_inc(uevac.handle, 1)
                    fn(U[:, c, P:512], Z[c % 2][:, P:512], ACT.Copy).then_inc(uevac.handle, 1)

            def kv_copies(g, blk):
                for c in range(C):
                    act.wait_ge(kvtr.handle, kvtr.at(g, blk, c + 1))
                    fn(kv[:, c, :], Z[c % 2][:], ACT.Copy).then_inc(kvevac.handle, 1)

            def state_copy(g, blk):
                act.wait_ge(sktr.handle, sktr.at(g, blk, 1))
                fn(Sk[:].rearrange("p c m -> p (c m)"), Z[0][:], ACT.Copy).then_inc(skevac.handle, 1)

            def softmax(g, blk):
                act.wait_ge(nmax.handle, nmax.at(g, blk, 1))
                for c in range(C):
                    fn(a[:, c, :], Z[0][:, c * P:(c + 1) * P], ACT.Exp, bias=nm[:, c:c + 1], scale=SC,
                       accum_out=den[:, c:c + 1]).then_inc(sexp.handle, 1)

            def gate(g, blk):
                if blk == 0:
                    act.wait_ge(wos_set, g + 1)
                act.wait_ge(ogs.handle, ogs.at(g, blk - 1, 1))
                act.wait_ge(gps.handle, gps.at(g, blk, 1))
                fn(gt[:], X[0][:], ACT.Tanh, bias=bgh[:, 0:1], scale=0.5).then_inc(gth.handle, 1)

            def o_square(g, blk):
                act.wait_ge(ogs.handle, ogs.at(g, blk, 1))
                fn(osq[:], O[:], ACT.Square).then_inc(osqs.handle, 1)

            def front_b(g, blk):
                kv_copies(g, blk)
                u_copies(g, blk)
                state_copy(g, blk)

            def first():
                evacuate(0, 0, 0)
                half_tanh(0, 0, 0)
                for i in range(4):
                    decays(0, 0, i)
                    if i == 0:
                        w_square(0, 0)
                    if i > 0:
                        evacuate(0, 0, i)
                        half_tanh(0, 0, i)
                pack_q(0, 0)
                pack_v(0, 0)
                front_b(0, 0)

            def slot(g, blk, more):
                gate(g, blk)
                if more:
                    evacuate(g, blk + 1, 0)
                softmax(g, blk)
                if more:
                    evacuate(g, blk + 1, 1)
                    half_tanh(g, blk + 1, 0)
                    decays(g, blk + 1, 0)
                    w_square(g, blk + 1)
                    evacuate(g, blk + 1, 2)
                    half_tanh(g, blk + 1, 1)
                o_square(g, blk)
                if more:
                    decays(g, blk + 1, 1)
                    evacuate(g, blk + 1, 3)
                    half_tanh(g, blk + 1, 2)
                    decays(g, blk + 1, 2)
                    decays(g, blk + 1, 3)
                    pack_q(g, blk + 1)
                    half_tanh(g, blk + 1, 3)
                    pack_v(g, blk + 1)
                    front_b(g, blk + 1)

            run(act, slot, first)

            act.wait_ge(f_tr, 1)
            fn(fwT[:].rearrange("p k n -> p (k n)"), Z[0][:].bitcast(BF16)[:, 0:512], ACT.Copy).then_inc(f_trc, 1)
            with act.Fori(0, BLOCKS) as i:
                act.wait_ge(f_tr, i + 2)
                fn(fqT[:].rearrange("p c k n -> p (c k n)"), Z[1][:].bitcast(BF16), ACT.Copy).then_inc(f_trc, 1)

        @block.vector
        def _(dve):
            v = nc.vector
            TT, TS, STT = v.tensor_tensor, v.tensor_scalar, v.scalar_tensor_tensor

            v.memset(ones[:], 1.0)
            v.memset(half[:], -0.5).then_inc(ones_set, 1)
            dve.wait_ge(const_in, 16 * 9)
            TS(nwh[:], nw[:], 0.5, None, ALU.mult).then_inc(ones_set, 1)
            v.tensor_copy(eyeb[:], eye[:]).then_inc(ones_set, 1)
            v.tensor_copy(msr[:], msum[:]).then_inc(ones_set, 1)
            with dve.Fori(0, BLOCKS) as i:
                dve.wait_ge(x_in, i * 16 + 16)
                for c in range(C):
                    v.bn_stats(stat[:, c, :], xa[:, bass.ds(i * C + c, 1), :].rearrange("p o d -> p (o d)")
                               ).then_inc(pr_stat, 1)
                for c in range(C):
                    hold(dve, "dve", pr_stat, i * C + c + 1)
                    v.bn_aggr(mv[:, c, :], stat[:, c, :]).then_inc(pr_aggr, 1)
                dve.wait_ge(pr_aggr, i * C + C)
                TS(var[:], mv[:, :, 1], EPS, None, ALU.add).then_inc(pr_var, 1)
                dve.wait_ge(pr_rstd, i + 1)
                dve.wait_ge(pr_tr, i * 2)
                for c in range(C):
                    TS(hn[:, c, :], xa[:, bass.ds(i * C + c, 1), :].rearrange("p o d -> p (o d)"),
                       mv[:, c, 0:1], rstd[:, c:c + 1], ALU.subtract, ALU.mult).then_inc(pr_h, 1)
                dve.wait_ge(pr_st, i * 32)
                dve.wait_ge(pr_beta, i)
                dve.wait_ge(pr_z, i * 16)
                for k in range(KT):
                    dve.wait_ge(pr_tr, i * 2 + k + 1)
                    v.tensor_copy(hTb[:, k, :], Z[k][:]).then_inc(pr_hT, 1)
                for j in range(2):
                    dve.wait_ge(pr_low, i * 2 + j + 1)
                    v.tensor_copy(low[:, j, :], X[j][:]).then_inc(pr_lowc, 1)
                dve.wait_ge(pr_beta, i + 1)
                v.tensor_copy(braw[:, :, bass.ds(i * C, C)],
                              O[:, 0:C * H].rearrange("p (c h) -> p h c", h=H)).then_inc(pr_betac, 1)
                dve.wait_ge(pr_sg, i * 128)
                for q in range(16):
                    c, j = q // 4, q % 4
                    dve.wait_ge(pr_z, i * 16 + q + 1)
                    TS(zs[:, c, j * 512:(j + 1) * 512], L[q % 2][:], ZMIN, None, ALU.max).then_inc(pr_zc, 1)
            dve.wait_ge(pr_tanh, 1)
            dve.wait_ge(pr_sg, BLOCKS * 128)
            dve.wait_ge(pr_st, BLOCKS * 32)
            TS(beta[:], beta[:], 1.0, 0.5, ALU.add, ALU.mult).then_inc(pr_bset, 1)
            dve.wait_ge(pr_bset, 1)
            for s_ in (conv, silu, cv, cnat, call, wprod, st0, stupd, aevac, prods, adds, smax, nmax, aes,
                       pevc, ogs, rsv, oacc):
                dve.sem_inc(s_.handle, 2 * s_.per)

            def taps(g, blk, i):
                w = ORDER[i]
                for j in range(3):
                    if j == 0:
                        dve.wait_ge(pevac.handle, pevac.at(g, blk, 2 * i + 2))
                    else:
                        dve.wait_ge(conv.handle, conv.at(g, blk, 3 * i + j))
                    STT(out=y[:, w, :], in0=xb[:, w, 1 + j:1 + j + NT], scalar=cw[:, w, j:j + 1], in1=y[:, w, :],
                        op0=ALU.mult, op1=ALU.add).then_inc(conv.handle, 1)

            def twice_silu(g, blk, i):
                w = ORDER[i]
                dve.wait_ge(tanh.handle, tanh.at(g, blk, i + 1))
                STT(out=y[:, w, :], in0=th[:, i % 2, :], scalar=1.0, in1=y[:, w, :], op0=ALU.add, op1=ALU.mult
                    ).then_inc(silu.handle, 1)

            def w_norm(g, blk):
                dve.wait_ge(wss.handle, wss.at(g, blk, 1))
                TS(cvv[:], S[:, 256:260], 4.0 * L2EPS, None, ALU.add).then_inc(cv.handle, 1)

            def w_factor(g, blk):
                dve.wait_ge(cpow.handle, cpow.at(g, blk, 1))
                h_at = g * (UN * C) + blk * C
                TT(cc[:, 2, :], cpw[:], beta[:].rearrange("p h c -> p (h c)")[:, bass.ds(h_at, C)], ALU.mult
                   ).then_inc(cnat.handle, 1)

            def w_factor_packed(g, blk):
                dve.wait_ge(cperm.handle, cperm.at(g, blk, 1))
                v.tensor_copy(cc[:, 0:2, :].rearrange("p q c -> p (q c)"), S[:, 260:268]).then_inc(call.handle, 1)

            def w_products(g, blk):
                dve.wait_ge(expA.handle, expA.at(g, blk, 8))
                dve.wait_ge(expB.handle, expB.at(g, blk, 4))
                EL = ELs[par(blk)]
                yw = y[:, 3, :]
                ywc = yw.rearrange("p (c m) -> p c m", c=C)
                TT(EL[:, :, SUF:SUF + P], ywc, EL[:, :, SUF:SUF + P], ALU.mult).then_inc(wprod.handle, 1)
                for q, s in enumerate(LEVELS):
                    e = packed(EL, LEFT + 64 * q, s)
                    TT(e, left(yw, s), e, ALU.mult).then_inc(wprod.handle, 1)
                TT(EL[:, :, DNEG:DNEG + P], ywc, EL[:, :, DNEG:DNEG + P], ALU.mult).then_inc(wprod.handle, 1)

            def a_masks(g, blk):
                dve.wait_ge(mcs.handle, mcs.at(g, blk, 1))
                for c in range(C):
                    dve.wait_ge(qk.handle, qk.at(g, blk, c + 1))
                    TT(A[:, c, :], X[(c + 1) % 2][:, 0:384], mc[:, c, :], ALU.mult).then_inc(aevac.handle, 1)

            def start_state(g, blk):
                dve.wait_ge(ops.handle, ops.at(g, blk - 1, 1))
                if blk % UN == 0:
                    v.memset(ST[:, 0, :], 0.0).then_inc(st0.handle, 1)
                else:
                    dve.wait_ge(stupd.handle, stupd.at(g, blk - 1, 4))
                    v.tensor_copy(ST[:, 0, :], ST[:, C, :]).then_inc(st0.handle, 1)

            def state_updates(g, blk):
                dve.wait_ge(st0.handle, st0.at(g, blk, 1))
                for c in range(C):
                    dve.wait_ge(stps.handle, stps.at(g, blk, c + 1))
                    if c > 0:
                        dve.wait_ge(stupd.handle, stupd.at(g, blk, c))
                    STT(out=ST[:, c + 1, :], in0=ST[:, c, :], scalar=ERs[par(blk)][:, c, P - 1:P], in1=S[:, 0:256],
                        op0=ALU.mult, op1=ALU.add).then_inc(stupd.handle, 1)

            def score_products(g, blk):
                for c in range(C):
                    dve.wait_ge(sc.handle, sc.at(g, blk, c + 1))
                    TT(pr[:, c, :], L[c % 2][:], ERs[par(blk)][:, c, :], ALU.mult).then_inc(prods.handle, 1)
                dve.wait_ge(prods.handle, prods.at(g, blk, 4))
                s_all = pr[:, :, 0:P]
                TT(s_all, s_all, pr[:, :, DPOS:DPOS + P], ALU.add).then_inc(adds.handle, 1)
                for q, s in enumerate(LEVELS):
                    dve.wait_ge(adds.handle, adds.at(g, blk, q + 1))
                    dst = s_all.rearrange("p c (n two s) -> p c n two s", two=2, s=s)[:, :, :, 1, :]
                    TT(dst, dst, packed(pr, RIGHT + 64 * q, s), ALU.add).then_inc(adds.handle, 1)

            def row_max(g, blk):
                dve.wait_ge(strn.handle, strn.at(g, blk, 1))
                v.tensor_reduce(out=mx[:], in_=Z[0][:].rearrange("p (c m) -> p c m", c=C), axis=AX.X, op=ALU.max
                                ).then_inc(smax.handle, 1)
                dve.wait_ge(smax.handle, smax.at(g, blk, 1))
                TS(nm[:], mx[:], -SC, None, ALU.mult).then_inc(nmax.handle, 1)

            def a_decays(g, blk):
                dve.wait_ge(atrn.handle, atrn.at(g, blk, 1))
                at = Z[1][:]
                ER = ERs[par(blk)]
                TT(AE[:, :, 0:256].rearrange("p c (w m) -> p c w m", w=2),
                   at.rearrange("p (c m) -> p c m", c=C).unsqueeze(2).broadcast_to([P, C, 2, P]),
                   ER[:, :, 0:256].rearrange("p c (w m) -> p c w m", w=2), ALU.mult).then_inc(aes.handle, 1)
                for q, s in enumerate(LEVELS):
                    TT(packed(AE, RIGHT + 64 * q, s), right(at, s), packed(ER, RIGHT + 64 * q, s), ALU.mult
                       ).then_inc(aes.handle, 1)

            def p_masks(g, blk):
                for c in range(C):
                    dve.wait_ge(pps.handle, pps.at(g, blk, c + 1))
                    TT(Pm[:, c, :], Z[c % 2][:, 0:384], mc[:, c, :], ALU.mult).then_inc(pevc.handle, 1)

            def o_gate(g, blk):
                dve.wait_ge(ops.handle, ops.at(g, blk, 1))
                dve.wait_ge(gth.handle, gth.at(g, blk, 1))
                STT(out=og[:], in0=gt[:], scalar=1.0, in1=O[:], op0=ALU.add, op1=ALU.mult).then_inc(ogs.handle, 1)

            def o_norm(g, blk):
                dve.wait_ge(sexp.handle, sexp.at(g, blk, 4))
                STT(out=r0[:], in0=den[:], scalar=4.0 * EPS, in1=den[:], op0=ALU.mult, op1=ALU.mult
                    ).then_inc(rsv.handle, 1)
                dve.wait_ge(rss.handle, rss.at(g, blk, 1))
                dve.wait_ge(rsv.handle, rsv.at(g, blk, 1))
                STT(out=r1[:], in0=S[:, 268:272], scalar=1.0 / P, in1=r0[:], op0=ALU.mult, op1=ALU.add
                    ).then_inc(rsv.handle, 1)

            def o_add(g, blk):
                dve.wait_ge(rpow.handle, rpow.at(g, blk, 1))
                for c in range(C):
                    if c % 2 == 0:
                        dve.wait_ge(wops.handle, wops.at(g, blk, c // 2 + 1))
                    xc = xa[:, bass.ds((g % 2) * (UN * C) + (blk * C + c), 1), :].rearrange("p o d -> p (o d)")
                    STT(out=xc, in0=Z[c // 2][:, (c % 2) * HID:(c % 2 + 1) * HID], scalar=rr[:, c:c + 1],
                        in1=xc, op0=ALU.mult, op1=ALU.add).then_inc(oacc.handle, 1)

            def front_b(g, blk):
                state_updates(g, blk)
                score_products(g, blk)

            def first():
                for i in range(4):
                    taps(0, 0, i)
                    twice_silu(0, 0, i)
                    if i == 1:
                        w_norm(0, 0)
                w_factor(0, 0)
                w_factor_packed(0, 0)
                start_state(0, 0)
                w_products(0, 0)
                a_masks(0, 0)
                front_b(0, 0)

            def slot(g, blk, more):
                row_max(g, blk)
                if more:
                    taps(g, blk + 1, 0)
                a_decays(g, blk)
                if more:
                    twice_silu(g, blk + 1, 0)
                p_masks(g, blk)
                if more:
                    taps(g, blk + 1, 1)
                o_gate(g, blk)
                if more:
                    w_norm(g, blk + 1)
                    twice_silu(g, blk + 1, 1)
                    w_factor(g, blk + 1)
                    taps(g, blk + 1, 2)
                o_norm(g, blk)
                if more:
                    twice_silu(g, blk + 1, 2)
                    taps(g, blk + 1, 3)
                o_add(g, blk)
                if more:
                    w_factor_packed(g, blk + 1)
                    start_state(g, blk + 1)
                    twice_silu(g, blk + 1, 3)
                    w_products(g, blk + 1)
                    a_masks(g, blk + 1)
                    front_b(g, blk + 1)

            run(dve, slot, first)

            dve.wait_ge(oacc.handle, oacc.at(GROUPS - 1, UN - 1, 4))
            with dve.Fori(0, BLOCKS) as i:
                for c in range(C):
                    v.bn_stats(fstat[:, c, :], xa[:, bass.ds(i * C + c, 1), :].rearrange("p o d -> p (o d)")
                               ).then_inc(f_stat, 1)
                for c in range(C):
                    hold(dve, "dve", f_stat, i * C + c + 1)
                    v.bn_aggr(fmv[:, c, :], fstat[:, c, :]).then_inc(f_aggr, 1)
                dve.wait_ge(f_aggr, i * C + C)
                TS(fvar[:], fmv[:, :, 1], EPS, None, ALU.add).then_inc(f_var, 1)
                dve.wait_ge(f_rstd, i + 1)
                for c in range(C):
                    TS(fy[:, bass.ds(i * C + c, 1), :].rearrange("p o d -> p (o d)"),
                       xa[:, bass.ds(i * C + c, 1), :].rearrange("p o d -> p (o d)"),
                       fmv[:, c, 0:1], frstd[:, c:c + 1], ALU.subtract, ALU.mult).then_inc(f_y, 1)
                dve.wait_ge(f_y, i * C + C)
                yblk = fy[:, bass.ds(i * C, C), :].rearrange("p c d -> p (c d)")
                v.tensor_reduce(out=fhi[:, bass.ds(i, 1)], in_=yblk, axis=AX.X, op=ALU.max).then_inc(f_mx, 1)
                v.tensor_reduce(out=flo[:, bass.ds(i, 1)], in_=yblk, axis=AX.X, op=ALU.min).then_inc(f_mx, 1)
            dve.wait_ge(f_in, 32)
            fwf = fw[:].rearrange("p a d -> p (a d)")
            v.tensor_reduce(out=fs[:, 0:1], in_=fwf, axis=AX.X, op=ALU.max).then_inc(f_wmx, 1)
            v.tensor_reduce(out=fs[:, 1:2], in_=fwf, axis=AX.X, op=ALU.min).then_inc(f_wmx, 1)
            dve.wait_ge(f_mx, 2 * BLOCKS)
            v.tensor_reduce(out=fs[:, 2:3], in_=fhi[:], axis=AX.X, op=ALU.max).then_inc(f_wmx, 1)
            v.tensor_reduce(out=fs[:, 3:4], in_=flo[:], axis=AX.X, op=ALU.min).then_inc(f_wmx, 1)
            dve.wait_ge(f_wmx, 4)
            STT(out=fs[:, 4:5], in0=fs[:, 3:4], scalar=-1.0, in1=fs[:, 2:3], op0=ALU.mult, op1=ALU.max
                ).then_inc(f_amax, 1)
            STT(out=fs[:, 5:6], in0=fs[:, 1:2], scalar=-1.0, in1=fs[:, 0:1], op0=ALU.mult, op1=ALU.max
                ).then_inc(f_amax, 1)
            dve.wait_ge(f_all, 1)
            TT(fs[:, 7:8], fs[:, 7:8], fs[:, 6:7], ALU.max).then_inc(f_sc, 1)
            dve.wait_ge(f_sc, 1)
            TS(fs[:, 8:10], fs[:, 6:8], 1.0 / QMAX, None, ALU.mult).then_inc(f_sc, 1)
            dve.wait_ge(f_sc, 2)
            v.reciprocal(fs[:, 10:12], fs[:, 8:10]).then_inc(f_sc, 1)
            TT(fs[:, 12:13], fs[:, 8:9], fs[:, 9:10], ALU.mult).then_inc(f_sc, 1)
            dve.wait_ge(f_sc, 4)

            quant_count = [0]

            def to_fp8(dst, src, inv, n, done, base):
                TS(fu[:, 0:n], src, inv, None, ALU.mult).then_inc(f_xb, 1)
                dve.wait_ge(f_xb, base + 1)
                TS(fm[:, 0:n].bitcast(U32), fu[:, 0:n].bitcast(U32), 0x7F800000, None, ALU.bitwise_and
                   ).then_inc(f_xb, 1)
                dve.wait_ge(f_xb, base + 2)
                TS(fm[:, 0:n], fm[:, 0:n], 2.0 ** -6, 1.5 * 2.0 ** 20, ALU.max, ALU.mult).then_inc(f_xb, 1)
                dve.wait_ge(f_xb, base + 3)
                TT(fu[:, 0:n], fu[:, 0:n], fm[:, 0:n], ALU.add).then_inc(f_xb, 1)
                dve.wait_ge(f_xb, base + 4)
                TT(dst, fu[:, 0:n], fm[:, 0:n], ALU.subtract).then_inc(done, 1)

            to_fp8(fwq[:].rearrange("p a d -> p (a d)"), fwf, fs[:, 11:12], KT * HID, f_wq, 0)
            dve.wait_ge(f_wq, 1)
            with dve.Fori(0, BLOCKS) as i:
                to_fp8(fq[:, bass.ds(i * C, C), :].rearrange("p c d -> p (c d)"),
                       fy[:, bass.ds(i * C, C), :].rearrange("p c d -> p (c d)"), fs[:, 10:11], C * HID, f_q,
                       i * (4 + C) + 4)
                dve.wait_ge(f_q, i + 1)
                for c in range(C):
                    xc = xa[:, bass.ds(i * C + c, 1), :].rearrange("p o d -> p (o d)")
                    TT(xc, xc, fb[:], ALU.add).then_inc(f_xb, 1)
                dve.wait_ge(f_mm, i + 1)
                dve.wait_ge(f_xb, i * (4 + C) + 8 + C)
                for c in range(C):
                    xc = xa[:, bass.ds(i * C + c, 1), :].rearrange("p o d -> p (o d)")
                    STT(out=xc, in0=X[c // 2][:, (c % 2) * HID:(c % 2 + 1) * HID], scalar=fs[:, 12:13], in1=xc,
                        op0=ALU.mult, op1=ALU.add).then_inc(f_out, 1)

        @block.gpsimd
        def _(pool):
            gp = nc.gpsimd
            pool.wait_ge(ones_set, 4)
            with pool.Fori(0, BLOCKS) as i:
                pool.wait_ge(pr_var, i + 1)
                gp.tensor_tensor(rstd[:], var[:], half[:], ALU.pow).then_inc(pr_rstd, 1)
            pool.wait_ge(pr_bset, 1)
            for s_ in (gpart, proj, kpacks, wss, cpow, cperm, mcs, lsum, utr, kvtr, stps, sktr, qk, sc, strn, atrn, pps,
                       ops, gps, rss, rpow, wops):
                pool.sem_inc(s_.handle, 2 * s_.per)

            def pack_k(g, blk):
                hold(pool, "pool", silu.handle, silu.at(g, blk, 2))
                for q, s in enumerate(LEVELS):
                    gp.tensor_copy(packed(pk[:, 0], 64 * q, s), left(y[:, 1, :], s)).then_inc(kpacks.handle, 1)

            def split_gates(g, blk):
                hold(pool, "pool", lsum.handle, lsum.at(g, blk - 1, 8))
                hold(pool, "pool", g_in[par(blk)], loads(g, blk))
                gp.tensor_copy(gh[:], gl[:, par(blk), :]).then_inc(gpart.handle, 1)
                pool.wait_ge(gpart.handle, gpart.at(g, blk, 1))
                gp.tensor_tensor(gr[:], gl[:, par(blk), :], gh[:].bitcast(F32), ALU.subtract
                                 ).then_inc(gpart.handle, 1)

            def w_power(g, blk):
                pool.wait_ge(cv.handle, cv.at(g, blk, 1))
                gp.tensor_tensor(cpw[:], cvv[:], half[:], ALU.pow).then_inc(cpow.handle, 1)

            def masks(g, blk):
                pool.wait_ge(call.handle, call.at(g, blk, 1))
                pool.wait_ge(pevc.handle, pevc.at(g, blk - 1, 4))
                gp.tensor_tensor(
                    mc[:].rearrange("p c (q m) -> p c q m", q=3),
                    mask[:].rearrange("p (q m) -> p q m", q=3).unsqueeze(1).broadcast_to([P, C, 3, P]),
                    cc[:].rearrange("p q c -> p c q").unsqueeze(3).broadcast_to([P, C, 3, P]),
                    ALU.mult).then_inc(mcs.handle, 1)

            def r_power(g, blk):
                pool.wait_ge(rsv.handle, rsv.at(g, blk, 2))
                gp.tensor_tensor(rr[:], r1[:], half[:], ALU.pow).then_inc(rpow.handle, 1)

            def out_weights(g):
                hold(pool, "pool", w2_in, g * 48 + 48)
                gp.tensor_scalar(bgh[:], bg[:], 0.5, None, ALU.mult)
                gp.tensor_scalar(wos[:], wo[:], nwh[:, 0:1], None, ALU.mult).then_inc(wos_set, 1)

            def first():
                split_gates(0, 0)
                w_power(0, 0)
                pack_k(0, 0)
                masks(0, 0)

            def slot(g, blk, more):
                if blk == 0:
                    out_weights(g)
                if more:
                    split_gates(g, blk + 1)
                    w_power(g, blk + 1)
                    pack_k(g, blk + 1)
                r_power(g, blk)
                if more:
                    masks(g, blk + 1)

            run(pool, slot, first)

            with pool.Fori(0, BLOCKS) as i:
                pool.wait_ge(f_var, i + 1)
                gp.tensor_tensor(frstd[:], fvar[:], half[:], ALU.pow).then_inc(f_rstd, 1)
            pool.wait_ge(f_amax, 2)
            gp.partition_all_reduce(fs[:, 6:8], fs[:, 4:6], P, RMAX).then_inc(f_all, 1)


def constants():
    import numpy as np

    i = np.arange(P)[:, None]
    t = np.arange(P)[None, :]

    def lefts(s):
        return np.array([j for j in range(P) if (j // s) % 2 == 0])

    def rights(s):
        return np.array([j for j in range(P) if (j // s) % 2 == 1])

    incl = (i <= t)
    ref = t // DIAG * DIAG + REF
    diag = ((i > ref) & (i <= t)).astype(np.float32) - ((i > t) & (i <= ref)).astype(np.float32)
    right = []
    left = []
    for s in LEVELS:
        r = rights(s)[None, :]
        right.append((i >= r // s * s) & (i <= r))
        q = lefts(s)[None, :]
        left.append((i > q) & (i < (q // s + 1) * s))
    suf = i > t
    msum = np.concatenate([incl, diag, *right, suf, *left], 1).astype(np.float32)

    mask = np.zeros((P, 384), np.float32)
    perm = np.zeros((P, 2, P), np.float32)
    for v, s in enumerate(LEVELS):
        q, h = v // 2, v % 2
        jl, tr_ = lefts(s), rights(s)
        same = (jl[:, None] // (2 * s)) == (tr_[None, :] // (2 * s))
        mask[h * 64:(h + 1) * 64, q * P + h * 64:q * P + (h + 1) * 64] = same
        perm[jl, q, h * 64 + np.arange(64)] = 1.0
    mask[:, 256:384] = (i <= t) & (i // DIAG == t // DIAG)
    return msum, mask, perm, np.eye(P, dtype=np.float32)


def kernel(**inputs):
    import numpy as np
    import concourse.bacc as bacc
    from concourse.bass_utils import run_bass_kernel_spmd

    def get(name):
        return np.ascontiguousarray(inputs["L0_" + name])

    def heads(w):
        return w.reshape(KT, P, H, P).transpose(2, 1, 0, 3)

    def taps(w):
        return w.reshape(H, P, TAPS)

    msum, mask, perm, eye = constants()
    wqkvw = np.stack([heads(get("attn_W" + n)) for n in "qkvw"], 3).reshape(H, P, KT * 4 * P)
    conv = np.stack([taps(get("attn_c" + n)) for n in "qkvv"], 2).reshape(H, P, 4 * TAPS)
    rows = lambda w: w.reshape(KT, P, -1).transpose(1, 0, 2)
    arrays = {
        "x": get("attn_hidden_states").reshape(TOK, HID),
        "wqkvw": wqkvw,
        "conv": conv,
        "wf1": rows(get("attn_Wf1")),
        "wf2": get("attn_Wf2"),
        "wb": rows(get("attn_Wb")),
        "wg1": rows(get("attn_Wg1")),
        "wg2": get("attn_Wg2").reshape(P, H, P).transpose(1, 0, 2),
        "bg": get("attn_bg2").reshape(H, P, 1),
        "nw": get("attn_norm_w").reshape(P, 1),
        "wo": get("attn_Wo").reshape(H, P, HID),
        "fw": get("ffn_weight"),
        "fb": get("ffn_bias"),
        "msum": msum,
        "mask": mask,
        "perm": perm,
        "eye": eye,
    }
    arrays = {k: np.ascontiguousarray(v) for k, v in arrays.items()}
    nc = bacc.Bacc("TRN2", target_bir_lowering=False, num_devices=1)
    args = [nc.dram_tensor("in_" + k, v.shape, mybir.dt.from_np(v.dtype), kind="ExternalInput").ap()
            for k, v in arrays.items()]
    out = nc.dram_tensor("out_0", (TOK, HID), F32, kind="ExternalOutput").ap()
    hT_d = nc.dram_tensor("hT_d", (BLOCKS, P, KT * NT), F32, kind="Internal").ap()
    h1_d = nc.dram_tensor("h1_d", (BLOCKS, P, NT), F32, kind="Internal").ap()
    g_d = nc.dram_tensor("g_d", (H, BLOCKS, P, NT), F32, kind="Internal").ap()
    program(nc, *args, out, hT_d, h1_d, g_d)
    r = run_bass_kernel_spmd(nc, [{"in_" + k: v for k, v in arrays.items()}], core_ids=[0])
    return r.results[0]["out_0"].reshape(TOK // SEQ, SEQ, HID)
```
